# Optimizing a Trainium2 kernel written in Bass

```python
import numpy as np
import jax
import jax.numpy as jnp

def _softmax(x, axis=-1):
    return jax.nn.softmax(x, axis=axis)

def _gelu(x):
    return jax.nn.gelu(x, approximate=True)

def _silu(x):
    return jax.nn.silu(x)

def _sigmoid(x):
    return jax.nn.sigmoid(x)

def _layernorm(x, axis=-1, eps=1e-05):
    m = jnp.mean(x, axis=axis, keepdims=True)
    v = jnp.var(x, axis=axis, keepdims=True)
    return (x - m) / jnp.sqrt(v + eps)

def _scatter_add(tgt, idx, src, axis=0):
    return tgt.at[idx].add(src)

def _segment_sum(src, seg, n):
    return jax.ops.segment_sum(src, seg, n)
kernel_name = 'mk_dlrm_tower_d1_rec_r8_124cbe'

def setup_inputs(seed: int=0):
    np.random.seed(seed)
    _w = jnp.asarray

    def _rec_inputs():
        import jax
        import jax.numpy as jnp
        _tk = jax.random.key(seed)
        dense_ctx = jax.random.normal(jax.random.fold_in(_tk, 190), (2048, 16), jnp.float32)
        ids = jnp.stack([jax.random.randint(jax.random.fold_in(_tk, 200 + f), (2048,), 0, v, jnp.int32) for f, v in enumerate([125000, 1000, 125000, 1000, 125000, 1000, 1000, 1000, 1250, 125000, 125000, 1250, 12500, 125000, 1000, 125000, 1250, 1000, 125000, 1250, 1000, 125000, 1000, 1250, 125000, 1250, 12500, 12500, 12500, 1000, 1250, 125000, 125000, 1000, 12500, 1250, 1000, 1250, 1000, 125000, 1000, 125000, 1250, 1250, 1000, 12500, 12500, 1250, 1000, 1250])], axis=1)
        tbl_0 = 0.05 * jax.random.normal(jax.random.fold_in(_tk, 500 + 0), (125000, 16), jnp.float32)
        tbl_1 = 0.05 * jax.random.normal(jax.random.fold_in(_tk, 500 + 1), (1000, 16), jnp.float32)
        tbl_2 = 0.05 * jax.random.normal(jax.random.fold_in(_tk, 500 + 2), (125000, 16), jnp.float32)
        tbl_3 = 0.05 * jax.random.normal(jax.random.fold_in(_tk, 500 + 3), (1000, 16), jnp.float32)
        tbl_4 = 0.05 * jax.random.normal(jax.random.fold_in(_tk, 500 + 4), (125000, 16), jnp.float32)
        tbl_5 = 0.05 * jax.random.normal(jax.random.fold_in(_tk, 500 + 5), (1000, 16), jnp.float32)
        tbl_6 = 0.05 * jax.random.normal(jax.random.fold_in(_tk, 500 + 6), (1000, 16), jnp.float32)
        tbl_7 = 0.05 * jax.random.normal(jax.random.fold_in(_tk, 500 + 7), (1000, 16), jnp.float32)
        tbl_8 = 0.05 * jax.random.normal(jax.random.fold_in(_tk, 500 + 8), (1250, 16), jnp.float32)
        tbl_9 = 0.05 * jax.random.normal(jax.random.fold_in(_tk, 500 + 9), (125000, 16), jnp.float32)
        tbl_10 = 0.05 * jax.random.normal(jax.random.fold_in(_tk, 500 + 10), (125000, 16), jnp.float32)
        tbl_11 = 0.05 * jax.random.normal(jax.random.fold_in(_tk, 500 + 11), (1250, 16), jnp.float32)
        tbl_12 = 0.05 * jax.random.normal(jax.random.fold_in(_tk, 500 + 12), (12500, 16), jnp.float32)
        tbl_13 = 0.05 * jax.random.normal(jax.random.fold_in(_tk, 500 + 13), (125000, 16), jnp.float32)
        tbl_14 = 0.05 * jax.random.normal(jax.random.fold_in(_tk, 500 + 14), (1000, 16), jnp.float32)
        tbl_15 = 0.05 * jax.random.normal(jax.random.fold_in(_tk, 500 + 15), (125000, 16), jnp.float32)
        tbl_16 = 0.05 * jax.random.normal(jax.random.fold_in(_tk, 500 + 16), (1250, 16), jnp.float32)
        tbl_17 = 0.05 * jax.random.normal(jax.random.fold_in(_tk, 500 + 17), (1000, 16), jnp.float32)
        tbl_18 = 0.05 * jax.random.normal(jax.random.fold_in(_tk, 500 + 18), (125000, 16), jnp.float32)
        tbl_19 = 0.05 * jax.random.normal(jax.random.fold_in(_tk, 500 + 19), (1250, 16), jnp.float32)
        tbl_20 = 0.05 * jax.random.normal(jax.random.fold_in(_tk, 500 + 20), (1000, 16), jnp.float32)
        tbl_21 = 0.05 * jax.random.normal(jax.random.fold_in(_tk, 500 + 21), (125000, 16), jnp.float32)
        tbl_22 = 0.05 * jax.random.normal(jax.random.fold_in(_tk, 500 + 22), (1000, 16), jnp.float32)
        tbl_23 = 0.05 * jax.random.normal(jax.random.fold_in(_tk, 500 + 23), (1250, 16), jnp.float32)
        tbl_24 = 0.05 * jax.random.normal(jax.random.fold_in(_tk, 500 + 24), (125000, 16), jnp.float32)
        tbl_25 = 0.05 * jax.random.normal(jax.random.fold_in(_tk, 500 + 25), (1250, 16), jnp.float32)
        tbl_26 = 0.05 * jax.random.normal(jax.random.fold_in(_tk, 500 + 26), (12500, 16), jnp.float32)
        tbl_27 = 0.05 * jax.random.normal(jax.random.fold_in(_tk, 500 + 27), (12500, 16), jnp.float32)
        tbl_28 = 0.05 * jax.random.normal(jax.random.fold_in(_tk, 500 + 28), (12500, 16), jnp.float32)
        tbl_29 = 0.05 * jax.random.normal(jax.random.fold_in(_tk, 500 + 29), (1000, 16), jnp.float32)
        tbl_30 = 0.05 * jax.random.normal(jax.random.fold_in(_tk, 500 + 30), (1250, 16), jnp.float32)
        tbl_31 = 0.05 * jax.random.normal(jax.random.fold_in(_tk, 500 + 31), (125000, 16), jnp.float32)
        tbl_32 = 0.05 * jax.random.normal(jax.random.fold_in(_tk, 500 + 32), (125000, 16), jnp.float32)
        tbl_33 = 0.05 * jax.random.normal(jax.random.fold_in(_tk, 500 + 33), (1000, 16), jnp.float32)
        tbl_34 = 0.05 * jax.random.normal(jax.random.fold_in(_tk, 500 + 34), (12500, 16), jnp.float32)
        tbl_35 = 0.05 * jax.random.normal(jax.random.fold_in(_tk, 500 + 35), (1250, 16), jnp.float32)
        tbl_36 = 0.05 * jax.random.normal(jax.random.fold_in(_tk, 500 + 36), (1000, 16), jnp.float32)
        tbl_37 = 0.05 * jax.random.normal(jax.random.fold_in(_tk, 500 + 37), (1250, 16), jnp.float32)
        tbl_38 = 0.05 * jax.random.normal(jax.random.fold_in(_tk, 500 + 38), (1000, 16), jnp.float32)
        tbl_39 = 0.05 * jax.random.normal(jax.random.fold_in(_tk, 500 + 39), (125000, 16), jnp.float32)
        tbl_40 = 0.05 * jax.random.normal(jax.random.fold_in(_tk, 500 + 40), (1000, 16), jnp.float32)
        tbl_41 = 0.05 * jax.random.normal(jax.random.fold_in(_tk, 500 + 41), (125000, 16), jnp.float32)
        tbl_42 = 0.05 * jax.random.normal(jax.random.fold_in(_tk, 500 + 42), (1250, 16), jnp.float32)
        tbl_43 = 0.05 * jax.random.normal(jax.random.fold_in(_tk, 500 + 43), (1250, 16), jnp.float32)
        tbl_44 = 0.05 * jax.random.normal(jax.random.fold_in(_tk, 500 + 44), (1000, 16), jnp.float32)
        tbl_45 = 0.05 * jax.random.normal(jax.random.fold_in(_tk, 500 + 45), (12500, 16), jnp.float32)
        tbl_46 = 0.05 * jax.random.normal(jax.random.fold_in(_tk, 500 + 46), (12500, 16), jnp.float32)
        tbl_47 = 0.05 * jax.random.normal(jax.random.fold_in(_tk, 500 + 47), (1250, 16), jnp.float32)
        tbl_48 = 0.05 * jax.random.normal(jax.random.fold_in(_tk, 500 + 48), (1000, 16), jnp.float32)
        tbl_49 = 0.05 * jax.random.normal(jax.random.fold_in(_tk, 500 + 49), (1250, 16), jnp.float32)
        _rk = jax.random.fold_in(_tk, 7)
        W_top1 = 0.0283866 * jax.random.normal(jax.random.fold_in(_tk, 801), (1241, 512), jnp.float32)
        W_top2 = 0.0441942 * jax.random.normal(jax.random.fold_in(_tk, 802), (512, 256), jnp.float32)
        W_top3 = 0.0625 * jax.random.normal(jax.random.fold_in(_tk, 803), (256, 1), jnp.float32)
        b_top1 = jnp.zeros((512,), jnp.float32)
        b_top2 = jnp.zeros((256,), jnp.float32)
        return (dense_ctx, ids, tbl_0, tbl_1, tbl_2, tbl_3, tbl_4, tbl_5, tbl_6, tbl_7, tbl_8, tbl_9, tbl_10, tbl_11, tbl_12, tbl_13, tbl_14, tbl_15, tbl_16, tbl_17, tbl_18, tbl_19, tbl_20, tbl_21, tbl_22, tbl_23, tbl_24, tbl_25, tbl_26, tbl_27, tbl_28, tbl_29, tbl_30, tbl_31, tbl_32, tbl_33, tbl_34, tbl_35, tbl_36, tbl_37, tbl_38, tbl_39, tbl_40, tbl_41, tbl_42, tbl_43, tbl_44, tbl_45, tbl_46, tbl_47, tbl_48, tbl_49, W_top1, b_top1, W_top2, b_top2, W_top3)
    dense_ctx, ids, tbl_0, tbl_1, tbl_2, tbl_3, tbl_4, tbl_5, tbl_6, tbl_7, tbl_8, tbl_9, tbl_10, tbl_11, tbl_12, tbl_13, tbl_14, tbl_15, tbl_16, tbl_17, tbl_18, tbl_19, tbl_20, tbl_21, tbl_22, tbl_23, tbl_24, tbl_25, tbl_26, tbl_27, tbl_28, tbl_29, tbl_30, tbl_31, tbl_32, tbl_33, tbl_34, tbl_35, tbl_36, tbl_37, tbl_38, tbl_39, tbl_40, tbl_41, tbl_42, tbl_43, tbl_44, tbl_45, tbl_46, tbl_47, tbl_48, tbl_49, W_top1, b_top1, W_top2, b_top2, W_top3 = _rec_inputs()

    def _L0_rec_setup():
        import jax, jax.numpy as jnp
        import numpy as np
        _NUM_FIELDS = 50
        _I_IDX, _J_IDX = np.triu_indices(_NUM_FIELDS, k=1)
        key = jax.random.key(seed)
        x = jax.random.normal(key, (2048, _NUM_FIELDS, 16), dtype=jnp.float32)
        return {'x': x}
    _L0_rec_all = _L0_rec_setup()
    _L0_rec_in = {k: v for k, v in _L0_rec_all.items() if k in ()}
    del _L0_rec_all
    return {'dense_ctx': dense_ctx, 'ids': ids, 'tbl_0': tbl_0, 'tbl_1': tbl_1, 'tbl_2': tbl_2, 'tbl_3': tbl_3, 'tbl_4': tbl_4, 'tbl_5': tbl_5, 'tbl_6': tbl_6, 'tbl_7': tbl_7, 'tbl_8': tbl_8, 'tbl_9': tbl_9, 'tbl_10': tbl_10, 'tbl_11': tbl_11, 'tbl_12': tbl_12, 'tbl_13': tbl_13, 'tbl_14': tbl_14, 'tbl_15': tbl_15, 'tbl_16': tbl_16, 'tbl_17': tbl_17, 'tbl_18': tbl_18, 'tbl_19': tbl_19, 'tbl_20': tbl_20, 'tbl_21': tbl_21, 'tbl_22': tbl_22, 'tbl_23': tbl_23, 'tbl_24': tbl_24, 'tbl_25': tbl_25, 'tbl_26': tbl_26, 'tbl_27': tbl_27, 'tbl_28': tbl_28, 'tbl_29': tbl_29, 'tbl_30': tbl_30, 'tbl_31': tbl_31, 'tbl_32': tbl_32, 'tbl_33': tbl_33, 'tbl_34': tbl_34, 'tbl_35': tbl_35, 'tbl_36': tbl_36, 'tbl_37': tbl_37, 'tbl_38': tbl_38, 'tbl_39': tbl_39, 'tbl_40': tbl_40, 'tbl_41': tbl_41, 'tbl_42': tbl_42, 'tbl_43': tbl_43, 'tbl_44': tbl_44, 'tbl_45': tbl_45, 'tbl_46': tbl_46, 'tbl_47': tbl_47, 'tbl_48': tbl_48, 'tbl_49': tbl_49, 'W_top1': W_top1, 'b_top1': b_top1, 'W_top2': W_top2, 'b_top2': b_top2, 'W_top3': W_top3}

def reference(dense_ctx, ids, tbl_0, tbl_1, tbl_2, tbl_3, tbl_4, tbl_5, tbl_6, tbl_7, tbl_8, tbl_9, tbl_10, tbl_11, tbl_12, tbl_13, tbl_14, tbl_15, tbl_16, tbl_17, tbl_18, tbl_19, tbl_20, tbl_21, tbl_22, tbl_23, tbl_24, tbl_25, tbl_26, tbl_27, tbl_28, tbl_29, tbl_30, tbl_31, tbl_32, tbl_33, tbl_34, tbl_35, tbl_36, tbl_37, tbl_38, tbl_39, tbl_40, tbl_41, tbl_42, tbl_43, tbl_44, tbl_45, tbl_46, tbl_47, tbl_48, tbl_49, W_top1, b_top1, W_top2, b_top2, W_top3):
    import jax
    import jax.numpy as jnp

    def _L0_rec_ref(x):
        import jax, jax.numpy as jnp
        import numpy as np
        _NUM_FIELDS = 50
        _I_IDX, _J_IDX = np.triu_indices(_NUM_FIELDS, k=1)
        gram = jnp.einsum('bid,bjd->bij', x, x)
        return gram[:, _I_IDX, _J_IDX]
    e = jnp.stack([tbl_0[ids[:, 0]], tbl_1[ids[:, 1]], tbl_2[ids[:, 2]], tbl_3[ids[:, 3]], tbl_4[ids[:, 4]], tbl_5[ids[:, 5]], tbl_6[ids[:, 6]], tbl_7[ids[:, 7]], tbl_8[ids[:, 8]], tbl_9[ids[:, 9]], tbl_10[ids[:, 10]], tbl_11[ids[:, 11]], tbl_12[ids[:, 12]], tbl_13[ids[:, 13]], tbl_14[ids[:, 14]], tbl_15[ids[:, 15]], tbl_16[ids[:, 16]], tbl_17[ids[:, 17]], tbl_18[ids[:, 18]], tbl_19[ids[:, 19]], tbl_20[ids[:, 20]], tbl_21[ids[:, 21]], tbl_22[ids[:, 22]], tbl_23[ids[:, 23]], tbl_24[ids[:, 24]], tbl_25[ids[:, 25]], tbl_26[ids[:, 26]], tbl_27[ids[:, 27]], tbl_28[ids[:, 28]], tbl_29[ids[:, 29]], tbl_30[ids[:, 30]], tbl_31[ids[:, 31]], tbl_32[ids[:, 32]], tbl_33[ids[:, 33]], tbl_34[ids[:, 34]], tbl_35[ids[:, 35]], tbl_36[ids[:, 36]], tbl_37[ids[:, 37]], tbl_38[ids[:, 38]], tbl_39[ids[:, 39]], tbl_40[ids[:, 40]], tbl_41[ids[:, 41]], tbl_42[ids[:, 42]], tbl_43[ids[:, 43]], tbl_44[ids[:, 44]], tbl_45[ids[:, 45]], tbl_46[ids[:, 46]], tbl_47[ids[:, 47]], tbl_48[ids[:, 48]], tbl_49[ids[:, 49]]], axis=1)
    z = _L0_rec_ref(e)
    z = z.reshape(z.shape[0], -1)
    h = jnp.concatenate([z, dense_ctx], axis=1)
    h = jnp.maximum(h @ W_top1 + b_top1, 0.0)
    h = jnp.maximum(h @ W_top2 + b_top2, 0.0)
    y = h @ W_top3
    return y

_drawn_inputs = setup_inputs


def setup_inputs(seed=0):
    import zlib

    import numpy as np

    out = dict(_drawn_inputs(seed))
    spreads = {'b_top1': (0.0, 0.1), 'b_top2': (0.0, 0.1)}
    factors = {'tbl_0': 5.28,
     'tbl_1': 5.064,
     'tbl_2': 4.573,
     'tbl_3': 4.888,
     'tbl_4': 4.547,
     'tbl_5': 5.155,
     'tbl_6': 4.591,
     'tbl_7': 4.628,
     'tbl_8': 4.946,
     'tbl_9': 4.733,
     'tbl_10': 4.869,
     'tbl_11': 4.682,
     'tbl_12': 4.651,
     'tbl_13': 4.652,
     'tbl_14': 4.907,
     'tbl_15': 4.546,
     'tbl_16': 5.106,
     'tbl_17': 4.425,
     'tbl_18': 5.122,
     'tbl_19': 5.033,
     'tbl_20': 4.705,
     'tbl_21': 4.83,
     'tbl_22': 4.947,
     'tbl_23': 5.099,
     'tbl_24': 4.853,
     'tbl_25': 4.969,
     'tbl_26': 4.868,
     'tbl_27': 5.177,
     'tbl_28': 4.673,
     'tbl_29': 5.063,
     'tbl_30': 5.446,
     'tbl_31': 5.581,
     'tbl_32': 5.003,
     'tbl_33': 4.868,
     'tbl_34': 5.439,
     'tbl_35': 4.65,
     'tbl_36': 4.569,
     'tbl_37': 4.85,
     'tbl_38': 4.752,
     'tbl_39': 4.706,
     'tbl_40': 4.711,
     'tbl_41': 4.776,
     'tbl_42': 4.966,
     'tbl_43': 4.809,
     'tbl_44': 4.942,
     'tbl_45': 4.851,
     'tbl_46': 4.626,
     'tbl_47': 4.145,
     'tbl_48': 4.981,
     'tbl_49': 4.876}
    for name, (base, spread) in spreads.items():
        noise = np.random.default_rng([zlib.crc32(name.encode()), seed]).standard_normal(out[name].shape)
        drawn = base * np.exp(spread * noise) if base else spread * noise
        out[name] = jnp.asarray(drawn.astype(out[name].dtype))
    for name, factor in factors.items():
        out[name] = (out[name] * factor).astype(out[name].dtype)
    return out
```

```python
from contextlib import ExitStack

import numpy as np
import concourse.bass as bass
from concourse import mybir

F32 = mybir.dt.float32
F16 = mybir.dt.float16
I32 = mybir.dt.int32
U32 = mybir.dt.uint32
ALU = mybir.AluOpType
ACT = mybir.ActivationFunctionType

B = 2048
DIM = 16
NF = 50
ND = 16
TILE = 128
TPC = 4
CHUNK = TILE * TPC
NCH = B // CHUNK
Q = 4
SPQ = TILE // Q
HALF = SPQ // 2
HB = Q * HALF
SCALE = 16.0

ROWS = [125000, 1000, 125000, 1000, 125000, 1000, 1000, 1000, 1250, 125000, 125000, 1250, 12500,
        125000, 1000, 125000, 1250, 1000, 125000, 1250, 1000, 125000, 1000, 1250, 125000, 1250,
        12500, 12500, 12500, 1000, 1250, 125000, 125000, 1000, 12500, 1250, 1000, 1250, 1000,
        125000, 1000, 125000, 1250, 1250, 1000, 12500, 12500, 1250, 1000, 1250]
SMALL_SIZES = (1000, 1250)
SMALL = [f for size in SMALL_SIZES for f in range(NF) if ROWS[f] == size]
BIG = [f for f in range(NF) if ROWS[f] not in SMALL_SIZES]
FIELD = SMALL + BIG
NS, NB = len(SMALL), len(BIG)
TP = 125
KS = [ROWS[f] // TP for f in SMALL]
KOFF = [sum(KS[:j]) for j in range(NS)]
KSUM = sum(KS)
KMAX = max(KS)
GRP = 4
NG = -(-NS // GRP)
NMASK = 3
JJ = NF // 2
JS = NS // 2
WORDS = 2 * DIM

ST = 11
TOP = 5
PIECES = []
_p = 0
for _g in range(4):
    _r = ST * _g + TOP + 1
    PIECES.append((_r, NF - _r, ST * _g, ST, _p, 0))
    _p += NF - _r
TOP_P = _p
for _g in range(5):
    PIECES.append((ST * _g + 1, TOP, ST * _g, TOP, TOP_P + TOP * (_g // 2), TOP * (_g % 2)))
DENSE_P = TOP_P + 3 * TOP
DENSE_R = 2
DENSE_K = ND // DENSE_R
KP = DENSE_P + DENSE_R
NCOL = NF - 1
HID1, HID2 = 512, 256
N1, N2 = HID1 // 128, HID2 // 128
MB = 2 * TILE

GROUPS_OF_TILE = [(0, 1), (2, 3), (4,), (5,)]
GROUPS_LAST = (6, 7)

PIECE_INC = 16 * len(PIECES)
GATHER_INC = 16 * NB
GRAM_CREDIT = 16
EVAC_CREDIT = 2
MLP_CREDIT = 8
MLPE_CREDIT = 4
MASK_CREDIT = 3
OH_CREDIT = 2
IDB_CREDIT = 2


def tables_of(q):
    return range(q * GRP, min(NS, (q + 1) * GRP))


def tables_back(j):
    return next(b for b in range(j + 1, NS) if (NS + j - b) % NMASK == j % NMASK)


def build(nc, small, big, ids_small, ids_big, dense, w1, b1, w2, b2, w3, y):
    ctx = ExitStack()
    with ctx:
        def sb(name, shape, dt):
            return ctx.enter_context(nc.sbuf_tensor(name, shape, dt))

        def sem(name):
            return ctx.enter_context(nc.semaphore(name))

        ids16_dram = nc.dram_tensor("ids16_dram", (NS, B), F16).ap()

        parts = sb("parts", [128, KSUM, 2, DIM], F16)
        w1_sb = sb("w1_sb", [128, ST, HID1], F32)
        w2_sb = sb("w2_sb", [128, N1, HID2], F32)
        w3_sb = sb("w3_sb", [128, N2, 128], F32)
        w3_in = sb("w3_in", [128, N2], F32)
        b1_sb = sb("b1_sb", [128, N1], F32)
        b2_sb = sb("b2_sb", [128, N2], F32)
        rows = sb("rows", [128, len(SMALL_SIZES), KMAX], F32)
        ids_bc = sb("ids_bc", [128, 2, GRP, CHUNK], F16)
        onehot = sb("onehot", [128, NMASK, KMAX, CHUNK], F16)
        looked = sb("looked", [128, NG, TPC, 2, WORDS, 2], F16)
        gidx = sb("gidx", [128, TPC, NB], I32)
        emb = sb("emb", [128, TPC, NB, DIM], F32)
        split = sb("split", [128, TPC, JJ, 3, DIM, 2], F16)
        TLEN = SPQ * NF
        turned = sb("turned", [128, 2, TLEN + 80], F16)
        turned2 = sb("turned2", [128, 2, TLEN + 80], F16)
        diag = sb("diag", [128, 2, HALF, Q, NF], F16)
        gram = sb("gram", [128, 2, NCOL * HB], F32)
        z = sb("z", [128, 2, ST, MB], F32)
        h1 = sb("h1", [128, N1, MB], F32)
        h2 = sb("h2", [128, N2, MB], F32)
        y_sb = sb("y_sb", [1, 2, MB], F32)

        stage = gram[:, :, :].rearrange("p a n -> p (a n)")
        small_f32 = stage[0:TP, 0:KSUM * DIM]
        ids_i32 = stage[0:NS, KSUM * DIM:KSUM * DIM + B].bitcast(I32)
        ids16 = diag[0:NS, :, :, :, :].rearrange("p a b c d -> p (a b c d)")[:, 0:B]

        gram_ps = [ctx.enter_context(nc.psum_tensor(f"gram_ps{i}", [128, 2, 512], F32)) for i in range(2)]
        look_ps = [ctx.enter_context(nc.psum_tensor(f"look_ps{i}", [128, 512], F32)) for i in range(2)]
        mlp_ps = [ctx.enter_context(nc.psum_tensor(f"mlp_ps{i}", [128, 512], F32)) for i in range(2)]

        ids_in = sem("ids_in")
        small_in = sem("small_in")
        ids_cast = sem("ids_cast")
        ids_saved = sem("ids_saved")
        weights_in = sem("weights_in")
        rows_made = sem("rows_made")
        cleared = sem("cleared")
        hi_made = sem("hi_made")
        parts_ready = sem("parts_ready")
        gidx_in = [sem(f"gidx_in{t}") for t in range(TPC)]
        gathered = [sem(f"gathered{t}") for t in range(TPC)]
        gathers_begun = sem("gathers_begun")
        emb_read = sem("emb_read")
        ids_bc_in = [sem(f"ids_bc_in{i}") for i in range(2)]
        ids_bc_used = sem("ids_bc_used")
        onehot_ready = sem("onehot_ready")
        onehot_used = sem("onehot_used")
        looked_ready = sem("looked_ready")
        looked_taken = sem("looked_taken")
        dve_step = sem("dve_step")
        diag_ready = sem("diag_ready")
        gram_done = sem("gram_done")
        gram_copied = sem("gram_copied")
        packed = [sem(f"packed{h}") for h in range(2)]
        dense_in = [sem(f"dense_in{i}") for i in range(2)]
        mlp_done = sem("mlp_done")
        mlp_copied = sem("mlp_copied")
        y_out = [sem(f"y_out{i}") for i in range(2)]

        block = ctx.enter_context(nc.Block())

        @block.sync
        def _(sp):
            def load_ids_bc(n, q):
                sp.wait_ge(ids_bc_used, n * NG + (q + IDB_CREDIT - 1))
                cnt = len(tables_of(q))
                src = ids16_dram[q * GRP:q * GRP + cnt, bass.ds(n * CHUNK, CHUNK)]
                sp.dma_start(ids_bc[0:TP, q % 2, 0:cnt, :],
                             src.unsqueeze(0).broadcast_to([TP, cnt, CHUNK])).then_inc(ids_bc_in[q % 2], 16)

            def load_gidx(n, t):
                sp.dma_start(gidx[:, t, :], ids_big[bass.ds(n * TPC + t, 1), :, :].rearrange("a p f -> (a p) f"))\
                  .then_inc(gidx_in[t], 16)

            def pack(c, t, h):
                sp.wait_ge(gram_copied, c * (8 * TPC) + (8 * t + 4 * h + 4 + EVAC_CREDIT))
                src = gram[:, h, :].rearrange("p (j b) -> p j b", b=HB)
                col = (t % 2) * TILE + h * HB
                for r0, nr, c0, ncol, p0, k0 in PIECES:
                    sp.dma_start(z[p0:p0 + nr, t // 2, k0:k0 + ncol, col:col + HB],
                                 src[r0:r0 + nr, c0:c0 + ncol, :]).then_inc(packed[h], 16)

            def chunk(c, more):
                for t in range(TPC):
                    m = t // 2
                    if more:
                        for q in GROUPS_OF_TILE[t]:
                            load_ids_bc(c + 1, q)
                        if t == TPC - 1:
                            load_ids_bc(c + 1, GROUPS_LAST[0])
                    if t % 2 == 0:
                        sp.wait_ge(mlp_done, c * 8 + (4 * m + 2))
                        sp.dma_start(z[DENSE_P:KP, m, 0:DENSE_K, :],
                                     dense[:, :, bass.ds(c * CHUNK + m * MB, MB)]).then_inc(dense_in[m], 16)
                    pack(c, t, 0)
                    if more and t == TPC - 1:
                        load_ids_bc(c + 1, GROUPS_LAST[1])
                    pack(c, t, 1)
                    if more:
                        sp.wait_ge(gathered[t], c * GATHER_INC + GATHER_INC)
                        load_gidx(c + 1, t)

            sp.dma_start(ids_i32, ids_small).then_inc(ids_in, 16)
            for t in range(TPC):
                load_gidx(0, t)
            sp.dma_start(small_f32, small).then_inc(small_in, 16)
            for s, d in ((w1_sb[0:KP, :, :], w1), (w2_sb[:, :, :], w2), (b1_sb[:, :], b1), (b2_sb[:, :], b2),
                         (w3_in[:, :], w3)):
                sp.dma_start(s, d).then_inc(weights_in, 16)
            sp.wait_ge(ids_cast, 1)
            sp.dma_start(ids16_dram, ids16).then_inc(ids_saved, 16)
            sp.wait_ge(ids_saved, 16)
            for i in range(2):
                sp.sem_inc(packed[i], PIECE_INC)
            for q in range(NG):
                load_ids_bc(0, q)
            with sp.Fori(0, NCH - 1) as c:
                chunk(c, True)
            chunk(NCH - 1, False)

        @block.gpsimd
        def _(pool):
            def gathers(c, reuse):
                for t in range(TPC):
                    pool.wait_ge(gidx_in[t], c * 16 + 16)
                    if reuse:
                        pool.wait_ge(emb_read, c * TPC + (t + 1 - TPC))
                    pool.sem_inc(gathers_begun, 1)
                    for f in range(NB):
                        pool.indirect_dma_start(
                            emb[:, t, f, :], None, big[f],
                            bass.IndirectOffsetOnAxis(ap=gidx[:, t, f:f + 1], axis=0)).then_inc(gathered[t], 16)

            for s in range(len(SMALL_SIZES)):
                k = SMALL_SIZES[s] // TP
                last = nc.gpsimd.iota(rows[0:TP, s, 0:k], [[1, k]], base=0, channel_multiplier=k,
                                      allow_small_or_imprecise_dtypes=True)
            last.then_inc(rows_made, 1)
            gathers(0, False)
            with pool.Fori(1, NCH) as c:
                gathers(c, True)

        @block.vector
        def _(dve):
            def compare(n, q):
                dve.wait_ge(ids_bc_in[q % 2], n * (16 * NG // 2) + 16 * (q // 2 + 1))
                for j in tables_of(q):
                    back = NMASK if j >= NMASK else tables_back(j)
                    dve.wait_ge(onehot_used, n * NS + (j - back + 1 + MASK_CREDIT))
                    for k in range(KS[j]):
                        s = SMALL_SIZES.index(ROWS[SMALL[j]])
                        last = nc.vector.tensor_scalar(
                            onehot[0:TP, j % NMASK, k, :], ids_bc[0:TP, q % 2, j % GRP, :],
                            rows[0:TP, s, k:k + 1], None, ALU.is_equal)
                    last.then_inc(onehot_ready, 1)
                dve.wait_ge(onehot_ready, n * NS + tables_of(q)[-1] + 1)
                dve.sem_inc(ids_bc_used, 1)

            STEPS = 1 + 5 * TPC

            def take_lookups(c):
                dve.wait_ge(looked_ready, c * NG + (NG + OH_CREDIT))
                for q in range(NG - 1):
                    nc.vector.tensor_copy(
                        split[:, :, 2 * q:2 * q + 2, 0:2, :, :].rearrange("p t j s d a -> p t j (s d a)"),
                        looked[:, q, :, :, :, :].rearrange("p t j w a -> p t j (w a)"))
                nc.vector.tensor_copy(
                    split[:, :, JS, 0:2, :, 0].rearrange("p t s d -> p t (s d)"),
                    looked[:, NG - 1, :, :, :, :].rearrange("p t j w a -> p t (j w a)")[:, :, 0:WORDS])\
                    .then_inc(dve_step, 1)
                dve.wait_ge(dve_step, c * STEPS + 1)
                nc.vector.tensor_copy(
                    split[:, :, 0:JS, 2, :, :].rearrange("p t j d a -> p t j (d a)"),
                    split[:, :, 0:JS, 0, :, :].rearrange("p t j d a -> p t j (d a)")).then_inc(looked_taken, 1)

            def set_out(c, t):
                step = 1 + 5 * t
                dve.wait_ge(gathered[t], c * GATHER_INC + GATHER_INC)

                def of_parity(a):
                    j0 = JS + 1 - a
                    e = emb[:, t, 1 - a:NB:2, :]
                    return e, split[:, t, j0:JJ, 0, :, a], split[:, t, j0:JJ, 1, :, a]

                for a in range(2):
                    e, hi, lo = of_parity(a)
                    nc.vector.tensor_scalar(hi, e, SCALE, None, ALU.mult).then_inc(dve_step, 1)
                dve.wait_ge(dve_step, c * STEPS + (step + 2))
                e, hi, lo = of_parity(0)
                nc.vector.scalar_tensor_tensor(lo, e, SCALE, hi, ALU.mult, ALU.subtract)
                e, hi, lo = of_parity(1)
                nc.vector.scalar_tensor_tensor(lo, e, SCALE, hi, ALU.mult, ALU.subtract).then_inc(emb_read, 1)
                nc.vector.tensor_copy(
                    split[:, t, JS:JJ, 2, :, :].rearrange("p j d a -> p j (d a)"),
                    split[:, t, JS:JJ, 0, :, :].rearrange("p j d a -> p j (d a)")).then_inc(dve_step, 1)
                dve.wait_ge(dve_step, c * STEPS + (step + 3))
                dve.wait_ge(gram_done, c * (8 * TPC) + (8 * t + GRAM_CREDIT - 8))
                src = split[:, t, :, :, :, :].rearrange("p j s d a -> p j (s d a)").bitcast(U32)
                for buf, w0 in ((turned, 0), (turned2, DIM)):
                    out = buf[:, t % 2, 0:TLEN].bitcast(U32).rearrange("p (b j) -> p j b", j=JJ)
                    nc.vector.transpose(out, src[:, :, w0:w0 + WORDS]).then_inc(dve_step, 1)
                dve.wait_ge(dve_step, c * STEPS + (step + 5))
                for h in range(2):
                    dve.wait_ge(gram_done, c * (8 * TPC) + (8 * t + 4 * h + GRAM_CREDIT - 4))
                    for r in range(Q):
                        p = slice(32 * r, 32 * r + 32)
                        last = nc.vector.tensor_copy(
                            diag[p, h, :, r, :].bitcast(U32),
                            turned[p, t % 2, h * HALF * NF:(h + 1) * HALF * NF].bitcast(U32)
                            .rearrange("p (b j) -> p b j", j=JJ))
                    last.then_inc(diag_ready, 1)

            def chunk(c, more):
                take_lookups(c)
                for t in range(TPC):
                    set_out(c, t)
                    if more:
                        for q in GROUPS_OF_TILE[t]:
                            compare(c + 1, q)
                if more:
                    for q in GROUPS_LAST:
                        compare(c + 1, q)

            dve.sem_inc(ids_bc_used, IDB_CREDIT)
            nc.vector.memset(z[96:128, :, :, :], 0.0)
            nc.vector.memset(w3_sb[:, :, :], 0.0)
            nc.vector.memset(turned[:, :, TLEN:], 0.0)
            nc.vector.memset(turned2[:, :, TLEN:], 0.0).then_inc(cleared, 1)
            dve.wait_ge(ids_in, 16)
            nc.vector.tensor_copy(ids16, ids_i32).then_inc(ids_cast, 1)
            dve.wait_ge(small_in, 16)
            sm = small_f32.rearrange("p (k d) -> p k d", d=DIM)
            dve.wait_ge(hi_made, 1)
            nc.vector.scalar_tensor_tensor(parts[0:TP, :, 1, :], sm, SCALE, parts[0:TP, :, 0, :],
                                           ALU.mult, ALU.subtract).then_inc(parts_ready, 1)
            dve.wait_ge(ids_saved, 16)
            dve.wait_ge(cleared, 1)
            nc.vector.memset(diag[:, :, :, :, :], 0.0)
            dve.wait_ge(weights_in, 16 * 5)
            nc.vector.tensor_copy(w3_sb[:, :, 0], w3_in[:, :]).then_inc(cleared, 1)
            dve.wait_ge(cleared, 2)
            dve.wait_ge(rows_made, 1)
            for q in range(NG):
                compare(0, q)
            with dve.Fori(0, NCH - 1) as c:
                chunk(c, True)
            chunk(NCH - 1, False)

        @block.tensor
        def _(pe):
            def look_up(n, j):
                q = j // GRP
                if j % GRP == 0:
                    pe.wait_ge(looked_ready, n * NG + (q + OH_CREDIT - 1))
                pe.wait_ge(onehot_ready, n * NS + (j + 1))
                width = 2 * WORDS if q == NG - 1 else GRP * WORDS
                for t in range(TPC):
                    o = look_ps[q % 2][:, t * width + (j % GRP) * WORDS:t * width + (j % GRP + 1) * WORDS]
                    for k in range(KS[j]):
                        last = nc.tensor.matmul(o, onehot[0:TP, j % NMASK, k, t * TILE:(t + 1) * TILE],
                                                parts[0:TP, KOFF[j] + k, :, :].rearrange("p s d -> p (s d)"),
                                                start=(k == 0), stop=(k == KS[j] - 1))
                last.then_inc(onehot_used, 1)

            def dots(c, t, g):
                if g % 4 == 0:
                    pe.wait_ge(diag_ready, c * (2 * TPC) + (2 * t + g // 4 + 1))
                pe.wait_ge(gram_copied, c * (8 * TPC) + (8 * t + g + EVAC_CREDIT - 1))
                for i in range(4):
                    b = 4 * g + i
                    o = gram_ps[g % 2][:, i // 2, (i % 2) * Q * NF:(i % 2 + 1) * Q * NF]
                    moving = diag[:, g // 4, b % HALF, :, :].rearrange("p r n -> p (r n)")
                    nc.tensor.matmul(o, turned[:, t % 2, b * NF:b * NF + 128], moving, start=True, stop=False)
                    last = nc.tensor.matmul(o, turned2[:, t % 2, b * NF:b * NF + 128], moving,
                                            start=False, stop=True)
                last.then_inc(gram_done, 1)

            def mlp(c, m):
                base = 4 * m
                for h in range(2):
                    pe.wait_ge(packed[h], c * (TPC * PIECE_INC) + PIECE_INC * (2 * m + 3))
                pe.wait_ge(dense_in[m], c * 16 + 16)
                for n in range(N1):
                    if n % 2 == 0:
                        pe.wait_ge(mlp_copied, c * 8 + (base + n // 2 + MLPE_CREDIT - 1))
                    for k in range(ST):
                        last = nc.tensor.matmul(mlp_ps[n // 2][:, (n % 2) * MB:(n % 2 + 1) * MB],
                                                w1_sb[0:KP, k, n * 128:(n + 1) * 128], z[0:KP, m, k, :],
                                                start=(k == 0), stop=(k == ST - 1))
                    if n % 2 == 1:
                        last.then_inc(mlp_done, 1)
                pe.wait_ge(mlp_copied, c * 8 + (base + 2 + MLPE_CREDIT))
                for o in range(N2):
                    for n in range(N1):
                        last = nc.tensor.matmul(mlp_ps[0][:, o * MB:(o + 1) * MB],
                                                w2_sb[:, n, o * 128:(o + 1) * 128], h1[:, n, :],
                                                start=(n == 0), stop=(n == N1 - 1))
                last.then_inc(mlp_done, 1)
                pe.wait_ge(mlp_copied, c * 8 + (base + 3 + MLPE_CREDIT))
                for o in range(N2):
                    last = nc.tensor.matmul(mlp_ps[1][:, 0:MB], w3_sb[:, o, :], h2[:, o, :],
                                            start=(o == 0), stop=(o == N2 - 1))
                last.then_inc(mlp_done, 1)

            def chunk(c, more):
                for t in range(TPC):
                    js = [j for q in GROUPS_OF_TILE[t] for j in tables_of(q)]
                    for g in range(8):
                        dots(c, t, g)
                        if more:
                            for j in js[g * len(js) // 8:(g + 1) * len(js) // 8]:
                                look_up(c + 1, j)
                    if t == 2:
                        mlp(c, 0)
                if more:
                    for q in GROUPS_LAST:
                        for j in tables_of(q):
                            look_up(c + 1, j)
                mlp(c, 1)

            pe.sem_inc(gram_done, GRAM_CREDIT)
            pe.sem_inc(mlp_done, MLP_CREDIT)
            pe.sem_inc(onehot_used, MASK_CREDIT)
            pe.wait_ge(parts_ready, 1)
            for q in range(NG):
                for j in tables_of(q):
                    look_up(0, j)
            pe.wait_ge(weights_in, 16 * 5)
            pe.wait_ge(cleared, 2)
            with pe.Fori(0, NCH - 1) as c:
                chunk(c, True)
            chunk(NCH - 1, False)

        @block.scalar
        def _(act):
            def copy_dots(c, t, g):
                h = g // 4
                if g % 4 == 0:
                    act.wait_ge(packed[h], c * (TPC * PIECE_INC) + PIECE_INC * (t + 1))
                act.wait_ge(gram_done, c * (8 * TPC) + (8 * t + g + 1 + GRAM_CREDIT))
                src = gram_ps[g % 2][0:NF, :, 0:2 * Q * NF].rearrange("p k (b j) -> p j k b", j=NF)[:, 0:NCOL]
                out = gram[0:NF, h, :].rearrange("p (j b) -> p j b", b=HB)[:, :, (g % 4) * 16:(g % 4 + 1) * 16]\
                    .rearrange("p j (k b) -> p j k b", k=2)
                nc.scalar.activation(out, src, ACT.Copy, scale=1.0 / (SCALE * SCALE)).then_inc(gram_copied, 1)

            def copy_lookups(n, q):
                act.wait_ge(onehot_used, n * NS + (tables_of(q)[-1] + 1 + MASK_CREDIT))
                if q == 0:
                    act.wait_ge(looked_taken, n + 1)
                if q < NG - 1:
                    src = look_ps[q % 2][:, :].rearrange("p (n a w) -> p n w a", a=2, w=WORDS)
                    out = looked[:, q, :, :, :, :].rearrange("p t j w a -> p (t j) w a")
                else:
                    src = look_ps[q % 2][:, 0:TPC * 2 * WORDS].rearrange("p (t w) -> p t w", t=TPC)[:, :, 0:WORDS]
                    out = looked[:, q, :, :, :, :].rearrange("p t j w a -> p t (j w a)")[:, :, 0:WORDS]
                nc.scalar.activation(out, src, ACT.Copy).then_inc(looked_ready, 1)

            def copy_mlp(c, m):
                base = 4 * m + MLP_CREDIT
                for n in range(N1):
                    if n % 2 == 0:
                        act.wait_ge(mlp_done, c * 8 + (base + n // 2 + 1))
                    ins = nc.scalar.activation(h1[:, n, :], mlp_ps[n // 2][:, (n % 2) * MB:(n % 2 + 1) * MB],
                                               ACT.Relu, bias=b1_sb[:, n:n + 1])
                    if n % 2 == 1:
                        ins.then_inc(mlp_copied, 1)
                act.wait_ge(mlp_done, c * 8 + (base + 3))
                for o in range(N2):
                    ins = nc.scalar.activation(h2[:, o, :], mlp_ps[0][:, o * MB:(o + 1) * MB],
                                               ACT.Relu, bias=b2_sb[:, o:o + 1])
                ins.then_inc(mlp_copied, 1)
                act.wait_ge(mlp_done, c * 8 + (base + 4))
                act.wait_ge(y_out[m], c * 16 + 16)
                nc.scalar.activation(
                    y_sb[0:1, m, :].rearrange("p (t r b) -> p t b r", t=2, r=Q),
                    mlp_ps[1][0:1, 0:MB].rearrange("p (t b r) -> p t b r", t=2, r=Q), ACT.Copy)\
                    .then_inc(mlp_copied, 1)
                act.wait_ge(mlp_copied, c * 8 + (4 * m + 4 + MLPE_CREDIT))
                act.dma_start(y[:, bass.ds(c * CHUNK + m * MB, MB)], y_sb[0:1, m, :]).then_inc(y_out[m], 16)

            def chunk(c, more):
                for t in range(TPC):
                    js = [j for q in GROUPS_OF_TILE[t] for j in tables_of(q)]
                    for g in range(8):
                        copy_dots(c, t, g)
                        if more:
                            for j in js[g * len(js) // 8:(g + 1) * len(js) // 8]:
                                if j % GRP == GRP - 1:
                                    copy_lookups(c + 1, j // GRP)
                    if t == 2:
                        copy_mlp(c, 0)
                if more:
                    for q in GROUPS_LAST:
                        copy_lookups(c + 1, q)
                copy_mlp(c, 1)

            act.sem_inc(gram_copied, EVAC_CREDIT)
            act.sem_inc(mlp_copied, MLPE_CREDIT)
            act.sem_inc(looked_ready, OH_CREDIT)
            act.sem_inc(looked_taken, 1)
            for i in range(2):
                act.sem_inc(y_out[i], 16)
            act.wait_ge(small_in, 16)
            nc.scalar.activation(parts[0:TP, :, 0, :], small_f32.rearrange("p (k d) -> p k d", d=DIM),
                                 ACT.Copy, scale=SCALE).then_inc(hi_made, 1)
            for q in range(NG):
                copy_lookups(0, q)
            act.wait_ge(parts_ready, 1)
            act.wait_ge(ids_cast, 1)
            act.wait_ge(weights_in, 16 * 5)
            with act.Fori(0, NCH - 1) as c:
                chunk(c, True)
            chunk(NCH - 1, False)
            for i in range(2):
                act.wait_ge(y_out[i], 16 * (NCH + 1))


def pair_rows():
    zero = NF * (NF - 1) // 2 + ND
    at = np.full((KP, ST), zero)
    seen = 0
    for r0, nr, c0, ncol, p0, k0 in PIECES:
        for r in range(nr):
            for k in range(ncol):
                if c0 + k < r0 + r:
                    i, j = sorted((FIELD[c0 + k], FIELD[r0 + r]))
                    at[p0 + r, k0 + k] = i * (2 * NF - i - 1) // 2 + j - i - 1
                    seen += 1
    assert seen == NF * (NF - 1) // 2
    for d in range(ND):
        at[DENSE_P + d // DENSE_K, d % DENSE_K] = NF * (NF - 1) // 2 + d
    return at


def kernel(**inputs):
    import concourse.bacc as bacc
    from concourse.bass_utils import run_bass_kernel_spmd

    a = {k: np.asarray(v) for k, v in inputs.items()}
    ids = a["ids"]
    small = np.concatenate([a[f"tbl_{f}"].reshape(TP, -1) for f in SMALL], axis=1)
    w1 = np.concatenate([a["W_top1"], np.zeros((1, HID1), np.float32)])[pair_rows()]
    dense = a["dense_ctx"].reshape(B // TILE, Q, SPQ, ND).transpose(3, 0, 2, 1).reshape(DENSE_R, DENSE_K, B)
    arrays = {
        "small": small,
        "ids_small": ids[:, SMALL].T,
        "ids_big": ids[:, BIG].reshape(B // TILE, TILE, NB),
        "dense": dense,
        "w1": w1,
        "b1": a["b_top1"].reshape(N1, 128).T,
        "w2": a["W_top2"].reshape(N1, 128, HID2).transpose(1, 0, 2),
        "b2": a["b_top2"].reshape(N2, 128).T,
        "w3": a["W_top3"].reshape(N2, 128).T,
    }
    for f in BIG:
        arrays[f"tbl_{f}"] = a[f"tbl_{f}"]
    arrays = {k: np.ascontiguousarray(v) for k, v in arrays.items()}
    nc = bacc.Bacc("TRN2", target_bir_lowering=False, num_devices=1)
    ap = {k: nc.dram_tensor(k, v.shape, mybir.dt.from_np(v.dtype), kind="ExternalInput").ap()
          for k, v in arrays.items()}
    y = nc.dram_tensor("y", (1, B), F32, kind="ExternalOutput").ap()
    build(nc, ap["small"], [ap[f"tbl_{f}"] for f in BIG], ap["ids_small"], ap["ids_big"], ap["dense"],
          ap["w1"], ap["b1"], ap["w2"], ap["b2"], ap["w3"], y)
    r = run_bass_kernel_spmd(nc, [arrays], core_ids=[0])
    return r.results[0]["y"].reshape(B, 1)
```

```python
from contextlib import ExitStack

import numpy as np
import concourse.bass as bass
from concourse import mybir

F32 = mybir.dt.float32
F16 = mybir.dt.float16
I32 = mybir.dt.int32
U32 = mybir.dt.uint32
ALU = mybir.AluOpType
ACT = mybir.ActivationFunctionType

B = 2048
DIM = 16
NF = 50
ND = 16
TILE = 128
TPC = 4
CHUNK = TILE * TPC
NCH = B // CHUNK
Q = 4
SPQ = TILE // Q
HALF = SPQ // 2
HB = Q * HALF
SCALE = 16.0

ROWS = [125000, 1000, 125000, 1000, 125000, 1000, 1000, 1000, 1250, 125000, 125000, 1250, 12500,
        125000, 1000, 125000, 1250, 1000, 125000, 1250, 1000, 125000, 1000, 1250, 125000, 1250,
        12500, 12500, 12500, 1000, 1250, 125000, 125000, 1000, 12500, 1250, 1000, 1250, 1000,
        125000, 1000, 125000, 1250, 1250, 1000, 12500, 12500, 1250, 1000, 1250]
SMALL_SIZES = (1000, 1250)
SMALL = [f for size in SMALL_SIZES for f in range(NF) if ROWS[f] == size]
BIG = [f for f in range(NF) if ROWS[f] not in SMALL_SIZES]
FIELD = SMALL + BIG
NS, NB = len(SMALL), len(BIG)
TP = 125
KS = [ROWS[f] // TP for f in SMALL]
KOFF = [sum(KS[:j]) for j in range(NS)]
KSUM = sum(KS)
KMAX = max(KS)
GRP = 4
NG = -(-NS // GRP)
SLICES = [KS[q * GRP] for q in range(NG)]
SOFF = [sum(SLICES[:q]) for q in range(NG + 1)]
NSL = SOFF[NG]
RING = 8
assert NSL % RING == 0 and all(KS[j] == SLICES[j // GRP] for j in range(NS))
WSCALE = 64.0
JJ = NF // 2
JS = NS // 2
WORDS = 2 * DIM

ST = 11
TOP = 5
PIECES = []
_p = 0
for _g in range(4):
    _r = ST * _g + TOP + 1
    PIECES.append((_r, NF - _r, ST * _g, ST, _p, 0))
    _p += NF - _r
TOP_P = _p
for _g in range(5):
    PIECES.append((ST * _g + 1, TOP, ST * _g, TOP, TOP_P + TOP * (_g // 2), TOP * (_g % 2)))
DENSE_P = TOP_P + 3 * TOP
DENSE_R = 2
DENSE_K = ND // DENSE_R
KP = DENSE_P + DENSE_R
NCOL = NF - 1
HID1, HID2 = 512, 256
N1, N2 = HID1 // 128, HID2 // 128
MB = 2 * TILE

ALL_SLICES = [(q, k) for q in range(NG) for k in range(SLICES[q])]
PER_TILE = NSL // TPC
IDS_BEFORE = ((0, 1), (3,), (5,), (7,))
IDS_BETWEEN = ((2,), (4,), (6,), ())


def slices_of(t, g):
    own = ALL_SLICES[t * PER_TILE:(t + 1) * PER_TILE]
    return own[g * PER_TILE // 8:(g + 1) * PER_TILE // 8]


PIECE_INC = 16 * len(PIECES)
GATHER_INC = 16 * NB
GRAM_CREDIT = 16
EVAC_CREDIT = 2
MLP_CREDIT = 8
MLPE_CREDIT = 4
HOT_CREDIT = RING
Z_CREDIT = 1
OH_CREDIT = 2


def tables_of(q):
    return range(q * GRP, min(NS, (q + 1) * GRP))


def build(nc, small, big, ids_small, ids_big, dense, w1, b1, w2, b2, w3, y):
    ctx = ExitStack()
    with ctx:
        def sb(name, shape, dt):
            return ctx.enter_context(nc.sbuf_tensor(name, shape, dt))

        def sem(name):
            return ctx.enter_context(nc.semaphore(name))

        ids16_dram = nc.dram_tensor("ids16_dram", (NS, B), F16).ap()

        parts = sb("parts", [128, KSUM, 2, DIM], F16)
        w1_sb = sb("w1_sb", [128, ST, 2, HID1], F16)
        w2_sb = sb("w2_sb", [128, N1, HID2], F32)
        w3_sb = sb("w3_sb", [128, N2, 128], F32)
        w3_in = sb("w3_in", [128, N2], F32)
        b1_sb = sb("b1_sb", [128, N1], F32)
        b2_sb = sb("b2_sb", [128, N2], F32)
        rows = sb("rows", [128, len(SMALL_SIZES), KMAX], F32)
        ids_bc = sb("ids_bc", [128, 2, GRP, CHUNK], F16)
        onehot = sb("onehot", [128, RING, GRP, CHUNK], F16)
        looked = sb("looked", [128, NG, TPC, 2, WORDS, 2], F16)
        gidx = sb("gidx", [128, TPC, NB], I32)
        emb = sb("emb", [128, TPC, NB, DIM], F32)
        split = sb("split", [128, TPC, JJ, 3, DIM, 2], F16)
        TLEN = SPQ * NF
        turned = sb("turned", [128, 2, TLEN + 80], F16)
        turned2 = sb("turned2", [128, 2, TLEN + 80], F16)
        diag = sb("diag", [128, 2, HALF, Q, NF], F16)
        gram = sb("gram", [128, 2, NCOL * HB], F32)
        z_both = sb("z_both", [128, 2, ST * MB], F32)
        z = z_both[:, 0, :].rearrange("p (k b) -> p k b", b=MB)
        z_parts = z_both[:, 1, :].bitcast(F16).rearrange("p (s k b) -> p s k b", s=2, b=MB)
        h1 = sb("h1", [128, N1, MB], F32)
        h2 = sb("h2", [128, N2, MB], F32)
        y_sb = sb("y_sb", [1, 2, MB], F32)

        stage = gram[:, :, :].rearrange("p a n -> p (a n)")
        w1_f32 = z_both[0:KP, :, :].rearrange("p a n -> p (a n)").rearrange("p (k n) -> p k n", n=HID1)
        small_f32 = stage[0:TP, 0:KSUM * DIM]
        ids_i32 = stage[0:NS, KSUM * DIM:KSUM * DIM + B].bitcast(I32)
        ids16 = diag[0:NS, :, :, :, :].rearrange("p a b c d -> p (a b c d)")[:, 0:B]

        gram_ps = [ctx.enter_context(nc.psum_tensor(f"gram_ps{i}", [128, 2, 512], F32)) for i in range(2)]
        look_ps = [ctx.enter_context(nc.psum_tensor(f"look_ps{i}", [128, 512], F32)) for i in range(2)]
        mlp_ps = [ctx.enter_context(nc.psum_tensor(f"mlp_ps{i}", [128, 512], F32)) for i in range(2)]

        ids_in = sem("ids_in")
        small_in = sem("small_in")
        ids_cast = sem("ids_cast")
        ids_saved = sem("ids_saved")
        weights_in = sem("weights_in")
        rows_made = sem("rows_made")
        cleared = sem("cleared")
        hi_made = sem("hi_made")
        parts_ready = sem("parts_ready")
        gidx_in = [sem(f"gidx_in{t}") for t in range(TPC)]
        gathered = [sem(f"gathered{t}") for t in range(TPC)]
        gathers_begun = sem("gathers_begun")
        emb_read = sem("emb_read")
        ids_bc_in = [sem(f"ids_bc_in{i}") for i in range(2)]
        onehot_ready = sem("onehot_ready")
        onehot_used = sem("onehot_used")
        looked_ready = sem("looked_ready")
        looked_taken = sem("looked_taken")
        dve_step = sem("dve_step")
        diag_ready = sem("diag_ready")
        gram_done = sem("gram_done")
        gram_copied = sem("gram_copied")
        w1_hi = sem("w1_hi")
        w1_ready = sem("w1_ready")
        z_hi = sem("z_hi")
        z_split = sem("z_split")
        packed = [sem(f"packed{h}") for h in range(2)]
        dense_in = sem("dense_in")
        mlp_done = sem("mlp_done")
        mlp_copied = sem("mlp_copied")
        y_out = [sem(f"y_out{i}") for i in range(2)]

        block = ctx.enter_context(nc.Block())

        @block.sync
        def _(sp):
            def load_ids_bc(n, q, first=False):
                if q >= 2:
                    sp.wait_ge(onehot_ready, n * NSL + SOFF[q - 1])
                elif not first:
                    sp.wait_ge(onehot_ready, n * NSL + (SOFF[NG + q - 1] - NSL))
                cnt = len(tables_of(q))
                src = ids16_dram[q * GRP:q * GRP + cnt, bass.ds(n * CHUNK, CHUNK)]
                sp.dma_start(ids_bc[0:TP, q % 2, 0:cnt, :],
                             src.unsqueeze(0).broadcast_to([TP, cnt, CHUNK])).then_inc(ids_bc_in[q % 2], 16)

            def load_gidx(n, t):
                sp.dma_start(gidx[:, t, :], ids_big[bass.ds(n * TPC + t, 1), :, :].rearrange("a p f -> (a p) f"))\
                  .then_inc(gidx_in[t], 16)

            def pack(c, t, h):
                sp.wait_ge(gram_copied, c * (8 * TPC) + (8 * t + 4 * h + 4 + EVAC_CREDIT))
                src = gram[:, h, :].rearrange("p (j b) -> p j b", b=HB)
                col = (t % 2) * TILE + h * HB
                for r0, nr, c0, ncol, p0, k0 in PIECES:
                    sp.dma_start(z[p0:p0 + nr, k0:k0 + ncol, col:col + HB],
                                 src[r0:r0 + nr, c0:c0 + ncol, :]).then_inc(packed[h], 16)

            def chunk(c, more):
                for t in range(TPC):
                    m = t // 2
                    if more:
                        for q in IDS_BEFORE[t]:
                            load_ids_bc(c + 1, q)
                    if t % 2 == 0:
                        sp.wait_ge(z_split, c * 2 + (m + Z_CREDIT))
                        sp.dma_start(z[DENSE_P:KP, 0:DENSE_K, :],
                                     dense[:, :, bass.ds(c * CHUNK + m * MB, MB)]).then_inc(dense_in, 16)
                    pack(c, t, 0)
                    if more:
                        for q in IDS_BETWEEN[t]:
                            load_ids_bc(c + 1, q)
                    pack(c, t, 1)
                    if more:
                        sp.wait_ge(gathered[t], c * GATHER_INC + GATHER_INC)
                        load_gidx(c + 1, t)

            sp.dma_start(ids_i32, ids_small).then_inc(ids_in, 16)
            for t in range(TPC):
                load_gidx(0, t)
            sp.dma_start(small_f32, small).then_inc(small_in, 16)
            for s, d in ((w1_f32, w1), (w2_sb[:, :, :], w2), (b1_sb[:, :], b1), (b2_sb[:, :], b2),
                         (w3_in[:, :], w3)):
                sp.dma_start(s, d).then_inc(weights_in, 16)
            sp.wait_ge(ids_cast, 1)
            sp.dma_start(ids16_dram, ids16).then_inc(ids_saved, 16)
            sp.wait_ge(ids_saved, 16)
            for i in range(2):
                sp.sem_inc(packed[i], PIECE_INC)
            for q in range(NG):
                load_ids_bc(0, q, first=True)
            sp.wait_ge(w1_ready, 1)
            with sp.Fori(0, NCH - 1) as c:
                chunk(c, True)
            chunk(NCH - 1, False)

        @block.gpsimd
        def _(pool):
            def gathers(c, reuse):
                for t in range(TPC):
                    pool.wait_ge(gidx_in[t], c * 16 + 16)
                    if reuse:
                        pool.wait_ge(emb_read, c * TPC + (t + 1 - TPC))
                    pool.sem_inc(gathers_begun, 1)
                    for f in range(NB):
                        pool.indirect_dma_start(
                            emb[:, t, f, :], None, big[f],
                            bass.IndirectOffsetOnAxis(ap=gidx[:, t, f:f + 1], axis=0)).then_inc(gathered[t], 16)

            for s in range(len(SMALL_SIZES)):
                k = SMALL_SIZES[s] // TP
                last = nc.gpsimd.iota(rows[0:TP, s, 0:k], [[1, k]], base=0, channel_multiplier=k,
                                      allow_small_or_imprecise_dtypes=True)
            last.then_inc(rows_made, 1)
            gathers(0, False)
            with pool.Fori(1, NCH) as c:
                gathers(c, True)

        @block.vector
        def _(dve):
            def compare(n, q, k):
                if k == 0:
                    dve.wait_ge(ids_bc_in[q % 2], n * (16 * NG // 2) + 16 * (q // 2 + 1))
                dve.wait_ge(onehot_used, n * NSL + (SOFF[q] + k + 1 - RING + HOT_CREDIT))
                cnt = len(tables_of(q))
                size = SMALL_SIZES.index(ROWS[SMALL[q * GRP]])
                nc.vector.tensor_scalar(onehot[0:TP, (SOFF[q] + k) % RING, 0:cnt, :], ids_bc[0:TP, q % 2, 0:cnt, :],
                                        rows[0:TP, size, k:k + 1], None, ALU.is_equal).then_inc(onehot_ready, 1)

            def split_products(c, m):
                dve.wait_ge(z_hi, c * 2 + (m + 1))
                nc.vector.tensor_tensor(z_parts[0:KP, 1, :, :], z[0:KP, :, :], z_parts[0:KP, 0, :, :],
                                        ALU.subtract).then_inc(z_split, 1)

            STEPS = 1 + 5 * TPC

            def take_lookups(c):
                dve.wait_ge(looked_ready, c * NG + (NG + OH_CREDIT))
                for q in range(NG - 1):
                    nc.vector.tensor_copy(
                        split[:, :, 2 * q:2 * q + 2, 0:2, :, :].rearrange("p t j s d a -> p t j (s d a)"),
                        looked[:, q, :, :, :, :].rearrange("p t j w a -> p t j (w a)"))
                nc.vector.tensor_copy(
                    split[:, :, JS, 0:2, :, 0].rearrange("p t s d -> p t (s d)"),
                    looked[:, NG - 1, :, :, :, :].rearrange("p t j w a -> p t (j w a)")[:, :, 0:WORDS])\
                    .then_inc(dve_step, 1)
                dve.wait_ge(dve_step, c * STEPS + 2)
                nc.vector.tensor_copy(
                    split[:, :, 0:JS, 2, :, :].rearrange("p t j d a -> p t j (d a)"),
                    split[:, :, 0:JS, 0, :, :].rearrange("p t j d a -> p t j (d a)")).then_inc(looked_taken, 1)

            def set_out(c, t):
                step = 2 + 5 * t
                dve.wait_ge(gathered[t], c * GATHER_INC + GATHER_INC)

                def of_parity(a):
                    j0 = JS + 1 - a
                    e = emb[:, t, 1 - a:NB:2, :]
                    return e, split[:, t, j0:JJ, 0, :, a], split[:, t, j0:JJ, 1, :, a]

                for a in range(2):
                    e, hi, lo = of_parity(a)
                    nc.vector.tensor_scalar(hi, e, SCALE, None, ALU.mult).then_inc(dve_step, 1)
                dve.wait_ge(dve_step, c * STEPS + (step + 2))
                e, hi, lo = of_parity(0)
                nc.vector.scalar_tensor_tensor(lo, e, SCALE, hi, ALU.mult, ALU.subtract)
                e, hi, lo = of_parity(1)
                nc.vector.scalar_tensor_tensor(lo, e, SCALE, hi, ALU.mult, ALU.subtract).then_inc(emb_read, 1)
                nc.vector.tensor_copy(
                    split[:, t, JS:JJ, 2, :, :].rearrange("p j d a -> p j (d a)"),
                    split[:, t, JS:JJ, 0, :, :].rearrange("p j d a -> p j (d a)")).then_inc(dve_step, 1)
                dve.wait_ge(dve_step, c * STEPS + (step + 3))
                dve.wait_ge(gram_done, c * (8 * TPC) + (8 * t + GRAM_CREDIT - 8))
                src = split[:, t, :, :, :, :].rearrange("p j s d a -> p j (s d a)").bitcast(U32)
                for buf, w0 in ((turned, 0), (turned2, DIM)):
                    out = buf[:, t % 2, 0:TLEN].bitcast(U32).rearrange("p (b j) -> p j b", j=JJ)
                    nc.vector.transpose(out, src[:, :, w0:w0 + WORDS]).then_inc(dve_step, 1)
                dve.wait_ge(dve_step, c * STEPS + (step + 5))
                for h in range(2):
                    dve.wait_ge(gram_done, c * (8 * TPC) + (8 * t + 4 * h + GRAM_CREDIT - 4))
                    for r in range(Q):
                        p = slice(32 * r, 32 * r + 32)
                        last = nc.vector.tensor_copy(
                            diag[p, h, :, r, :].bitcast(U32),
                            turned[p, t % 2, h * HALF * NF:(h + 1) * HALF * NF].bitcast(U32)
                            .rearrange("p (b j) -> p b j", j=JJ))
                    last.then_inc(diag_ready, 1)

            def chunk(c, before, more):
                take_lookups(c)
                for t in range(TPC):
                    set_out(c, t)
                    if t % 2 == 0 and (before or t > 0):
                        split_products(c, t // 2 - 1)
                    if more:
                        for g in range(8):
                            for q, k in slices_of(t, g):
                                compare(c + 1, q, k)

            dve.sem_inc(z_split, Z_CREDIT)
            nc.vector.memset(w3_sb[:, :, :], 0.0)
            nc.vector.memset(turned[:, :, TLEN:], 0.0)
            nc.vector.memset(turned2[:, :, TLEN:], 0.0).then_inc(cleared, 1)
            dve.wait_ge(ids_in, 16)
            nc.vector.tensor_copy(ids16, ids_i32).then_inc(ids_cast, 1)
            dve.wait_ge(ids_saved, 16)
            nc.vector.memset(diag[:, :, :, :, :], 0.0).then_inc(cleared, 1)
            dve.wait_ge(rows_made, 1)
            for q in range(NG):
                for k in range(SLICES[q]):
                    compare(0, q, k)
                if q == 0:
                    dve.wait_ge(hi_made, 1)
                    nc.vector.scalar_tensor_tensor(
                        parts[0:TP, :, 1, :], small_f32.rearrange("p (k d) -> p k d", d=DIM), SCALE,
                        parts[0:TP, :, 0, :], ALU.mult, ALU.subtract).then_inc(parts_ready, 1)
            dve.wait_ge(w1_hi, 1)
            nc.vector.tensor_copy(w3_sb[:, :, 0], w3_in[:, :])
            nc.vector.scalar_tensor_tensor(w1_sb[0:KP, :, 1, :], w1_f32, WSCALE, w1_sb[0:KP, :, 0, :],
                                           ALU.mult, ALU.subtract).then_inc(dve_step, 1)
            dve.wait_ge(dve_step, 1)
            nc.vector.memset(z[96:128, :, :], 0.0).then_inc(w1_ready, 1)
            chunk(0, False, True)
            with dve.Fori(1, NCH - 1) as c:
                chunk(c, True, True)
            chunk(NCH - 1, True, False)
            split_products(NCH - 1, 1)

        @block.tensor
        def _(pe):
            def look_up(n, q, k):
                if k == 0:
                    pe.wait_ge(looked_ready, n * NG + (q + OH_CREDIT - 1))
                pe.wait_ge(onehot_ready, n * NSL + (SOFF[q] + k + 1))
                width = 2 * WORDS if q == NG - 1 else GRP * WORDS
                js = tables_of(q)
                for j in js:
                    for t in range(TPC):
                        at = t * width + (j % GRP) * WORDS
                        last = nc.tensor.matmul(
                            look_ps[q % 2][:, at:at + WORDS],
                            onehot[0:TP, (SOFF[q] + k) % RING, j % GRP, t * TILE:(t + 1) * TILE],
                            parts[0:TP, KOFF[j] + k, :, :].rearrange("p s d -> p (s d)"),
                            start=(k == 0 and j == js[0] and t == 0),
                            stop=(k == SLICES[q] - 1), skip_group_check=True)
                last.then_inc(onehot_used, 1)

            def dots(c, t, g):
                if g % 4 == 0:
                    pe.wait_ge(diag_ready, c * (2 * TPC) + (2 * t + g // 4 + 1))
                pe.wait_ge(gram_copied, c * (8 * TPC) + (8 * t + g + EVAC_CREDIT - 1))
                for i in range(4):
                    b = 4 * g + i
                    o = gram_ps[g % 2][:, i // 2, (i % 2) * Q * NF:(i % 2 + 1) * Q * NF]
                    moving = diag[:, g // 4, b % HALF, :, :].rearrange("p r n -> p (r n)")
                    nc.tensor.matmul(o, turned[:, t % 2, b * NF:b * NF + 128], moving, start=True, stop=False)
                    last = nc.tensor.matmul(o, turned2[:, t % 2, b * NF:b * NF + 128], moving,
                                            start=False, stop=True)
                last.then_inc(gram_done, 1)

            def first_layer(c, m, part):
                if part == 0:
                    pe.wait_ge(z_split, c * 2 + (m + 1 + Z_CREDIT))
                pe.wait_ge(mlp_copied, c * 8 + (4 * m + part + MLPE_CREDIT - 1))
                for i in range(2):
                    n = 2 * part + i
                    for k in range(ST):
                        for w, x in ((0, 0), (0, 1), (1, 0)):
                            last = nc.tensor.matmul(mlp_ps[part][:, i * MB:(i + 1) * MB],
                                                    w1_sb[0:KP, k, w, n * 128:(n + 1) * 128],
                                                    z_parts[0:KP, x, k, :], start=(k == 0 and w + x == 0),
                                                    stop=(k == ST - 1 and w == 1))
                last.then_inc(mlp_done, 1)

            def last_layers(c, m):
                base = 4 * m
                pe.wait_ge(mlp_copied, c * 8 + (base + 2 + MLPE_CREDIT))
                for o in range(N2):
                    for n in range(N1):
                        last = nc.tensor.matmul(mlp_ps[0][:, o * MB:(o + 1) * MB],
                                                w2_sb[:, n, o * 128:(o + 1) * 128], h1[:, n, :],
                                                start=(n == 0), stop=(n == N1 - 1))
                last.then_inc(mlp_done, 1)
                pe.wait_ge(mlp_copied, c * 8 + (base + 3 + MLPE_CREDIT))
                for o in range(N2):
                    last = nc.tensor.matmul(mlp_ps[1][:, 0:MB], w3_sb[:, o, :], h2[:, o, :],
                                            start=(o == 0), stop=(o == N2 - 1))
                last.then_inc(mlp_done, 1)

            def chunk(c, before, more):
                for t in range(TPC):
                    for g in range(8):
                        dots(c, t, g)
                        if more:
                            for q, k in slices_of(t, g):
                                look_up(c + 1, q, k)
                    m = t // 2 - 1
                    if before or m >= 0:
                        first_layer(c, m, t % 2)
                        if t % 2 == 1:
                            last_layers(c, m)

            pe.sem_inc(gram_done, GRAM_CREDIT)
            pe.sem_inc(mlp_done, MLP_CREDIT)
            pe.sem_inc(onehot_used, HOT_CREDIT)
            pe.wait_ge(parts_ready, 1)
            for q in range(NG):
                for k in range(SLICES[q]):
                    look_up(0, q, k)
            pe.wait_ge(weights_in, 16 * 5)
            pe.wait_ge(cleared, 2)
            pe.wait_ge(w1_ready, 1)
            chunk(0, False, True)
            with pe.Fori(1, NCH - 1) as c:
                chunk(c, True, True)
            chunk(NCH - 1, True, False)
            first_layer(NCH - 1, 1, 0)
            first_layer(NCH - 1, 1, 1)
            last_layers(NCH - 1, 1)

        @block.scalar
        def _(act):
            def copy_dots(c, t, g):
                h = g // 4
                if g % 4 == 0:
                    act.wait_ge(packed[h], c * (TPC * PIECE_INC) + PIECE_INC * (t + 1))
                act.wait_ge(gram_done, c * (8 * TPC) + (8 * t + g + 1 + GRAM_CREDIT))
                src = gram_ps[g % 2][0:NF, :, 0:2 * Q * NF].rearrange("p k (b j) -> p j k b", j=NF)[:, 0:NCOL]
                out = gram[0:NF, h, :].rearrange("p (j b) -> p j b", b=HB)[:, :, (g % 4) * 16:(g % 4 + 1) * 16]\
                    .rearrange("p j (k b) -> p j k b", k=2)
                nc.scalar.activation(out, src, ACT.Copy, scale=1.0 / (SCALE * SCALE)).then_inc(gram_copied, 1)

            def copy_lookups(n, q):
                act.wait_ge(onehot_used, n * NSL + (SOFF[q + 1] + HOT_CREDIT))
                if q == 0:
                    act.wait_ge(looked_taken, n + 1)
                if q < NG - 1:
                    src = look_ps[q % 2][:, :].rearrange("p (n a w) -> p n w a", a=2, w=WORDS)
                    out = looked[:, q, :, :, :, :].rearrange("p t j w a -> p (t j) w a")
                else:
                    src = look_ps[q % 2][:, 0:TPC * 2 * WORDS].rearrange("p (t w) -> p t w", t=TPC)[:, :, 0:WORDS]
                    out = looked[:, q, :, :, :, :].rearrange("p t j w a -> p t (j w a)")[:, :, 0:WORDS]
                nc.scalar.activation(out, src, ACT.Copy).then_inc(looked_ready, 1)

            def split_products(c, m):
                for h in range(2):
                    act.wait_ge(packed[h], c * (TPC * PIECE_INC) + PIECE_INC * (2 * m + 3))
                act.wait_ge(dense_in, c * 32 + 16 * (m + 1))
                act.wait_ge(mlp_done, c * 8 + (4 * m + 2 + MLP_CREDIT - 4))
                nc.scalar.activation(z_parts[0:KP, 0, :, :], z[0:KP, :, :], ACT.Copy).then_inc(z_hi, 1)

            def copy_first_layer(c, m, part):
                act.wait_ge(mlp_done, c * 8 + (4 * m + part + 1 + MLP_CREDIT))
                for i in range(2):
                    n = 2 * part + i
                    ins = nc.scalar.activation(h1[:, n, :], mlp_ps[part][:, i * MB:(i + 1) * MB],
                                               ACT.Relu, bias=b1_sb[:, n:n + 1], scale=1.0 / WSCALE)
                ins.then_inc(mlp_copied, 1)

            def copy_last_layers(c, m):
                base = 4 * m + MLP_CREDIT
                act.wait_ge(mlp_done, c * 8 + (base + 3))
                for o in range(N2):
                    ins = nc.scalar.activation(h2[:, o, :], mlp_ps[0][:, o * MB:(o + 1) * MB],
                                               ACT.Relu, bias=b2_sb[:, o:o + 1])
                ins.then_inc(mlp_copied, 1)
                act.wait_ge(mlp_done, c * 8 + (base + 4))
                act.wait_ge(y_out[m % 2], c * 16 + (16 if m >= 0 else 0))
                nc.scalar.activation(
                    y_sb[0:1, m % 2, :].rearrange("p (t r b) -> p t b r", t=2, r=Q),
                    mlp_ps[1][0:1, 0:MB].rearrange("p (t b r) -> p t b r", t=2, r=Q), ACT.Copy)\
                    .then_inc(mlp_copied, 1)
                act.wait_ge(mlp_copied, c * 8 + (4 * m + 4 + MLPE_CREDIT))
                act.dma_start(y[:, bass.ds(c * CHUNK + m * MB, MB)], y_sb[0:1, m % 2, :]).then_inc(y_out[m % 2], 16)

            def chunk(c, before, more):
                for t in range(TPC):
                    m = t // 2 - 1
                    if t % 2 == 0 and (before or m >= 0):
                        split_products(c, m)
                    for g in range(8):
                        copy_dots(c, t, g)
                        if more:
                            for q, k in slices_of(t, g):
                                if k == SLICES[q] - 1:
                                    copy_lookups(c + 1, q)
                    if before or m >= 0:
                        copy_first_layer(c, m, t % 2)
                        if t % 2 == 1:
                            copy_last_layers(c, m)

            act.sem_inc(gram_copied, EVAC_CREDIT)
            act.sem_inc(mlp_copied, MLPE_CREDIT)
            act.sem_inc(looked_ready, OH_CREDIT)
            act.sem_inc(looked_taken, 1)
            for i in range(2):
                act.sem_inc(y_out[i], 16)
            act.wait_ge(small_in, 16)
            nc.scalar.activation(parts[0:TP, :, 0, :], small_f32.rearrange("p (k d) -> p k d", d=DIM),
                                 ACT.Copy, scale=SCALE).then_inc(hi_made, 1)
            for q in range(NG):
                copy_lookups(0, q)
                if q == 0:
                    act.wait_ge(weights_in, 16 * 5)
                    nc.scalar.activation(w1_sb[0:KP, :, 0, :], w1_f32, ACT.Copy, scale=WSCALE).then_inc(w1_hi, 1)
            act.wait_ge(parts_ready, 1)
            act.wait_ge(ids_cast, 1)
            chunk(0, False, True)
            with act.Fori(1, NCH - 1) as c:
                chunk(c, True, True)
            chunk(NCH - 1, True, False)
            split_products(NCH - 1, 1)
            copy_first_layer(NCH - 1, 1, 0)
            copy_first_layer(NCH - 1, 1, 1)
            copy_last_layers(NCH - 1, 1)
            for i in range(2):
                act.wait_ge(y_out[i], 16 * (NCH + 1))


def pair_rows():
    zero = NF * (NF - 1) // 2 + ND
    at = np.full((KP, ST), zero)
    seen = 0
    for r0, nr, c0, ncol, p0, k0 in PIECES:
        for r in range(nr):
            for k in range(ncol):
                if c0 + k < r0 + r:
                    i, j = sorted((FIELD[c0 + k], FIELD[r0 + r]))
                    at[p0 + r, k0 + k] = i * (2 * NF - i - 1) // 2 + j - i - 1
                    seen += 1
    assert seen == NF * (NF - 1) // 2
    for d in range(ND):
        at[DENSE_P + d // DENSE_K, d % DENSE_K] = NF * (NF - 1) // 2 + d
    return at


def kernel(**inputs):
    import concourse.bacc as bacc
    from concourse.bass_utils import run_bass_kernel_spmd

    a = {k: np.asarray(v) for k, v in inputs.items()}
    ids = a["ids"]
    small = np.concatenate([a[f"tbl_{f}"].reshape(TP, -1) for f in SMALL], axis=1)
    w1 = np.concatenate([a["W_top1"], np.zeros((1, HID1), np.float32)])[pair_rows()]
    dense = a["dense_ctx"].reshape(B // TILE, Q, SPQ, ND).transpose(3, 0, 2, 1).reshape(DENSE_R, DENSE_K, B)
    arrays = {
        "small": small,
        "ids_small": ids[:, SMALL].T,
        "ids_big": ids[:, BIG].reshape(B // TILE, TILE, NB),
        "dense": dense,
        "w1": w1,
        "b1": a["b_top1"].reshape(N1, 128).T,
        "w2": a["W_top2"].reshape(N1, 128, HID2).transpose(1, 0, 2),
        "b2": a["b_top2"].reshape(N2, 128).T,
        "w3": a["W_top3"].reshape(N2, 128).T,
    }
    for f in BIG:
        arrays[f"tbl_{f}"] = a[f"tbl_{f}"]
    arrays = {k: np.ascontiguousarray(v) for k, v in arrays.items()}
    nc = bacc.Bacc("TRN2", target_bir_lowering=False, num_devices=1)
    ap = {k: nc.dram_tensor(k, v.shape, mybir.dt.from_np(v.dtype), kind="ExternalInput").ap()
          for k, v in arrays.items()}
    y = nc.dram_tensor("y", (1, B), F32, kind="ExternalOutput").ap()
    build(nc, ap["small"], [ap[f"tbl_{f}"] for f in BIG], ap["ids_small"], ap["ids_big"], ap["dense"],
          ap["w1"], ap["b1"], ap["w2"], ap["b2"], ap["w3"], y)
    r = run_bass_kernel_spmd(nc, [arrays], core_ids=[0])
    return r.results[0]["y"].reshape(B, 1)
```

```python
from contextlib import ExitStack

import numpy as np
import concourse.bass as bass
from concourse import mybir

F32 = mybir.dt.float32
F16 = mybir.dt.float16
I32 = mybir.dt.int32
U32 = mybir.dt.uint32
ALU = mybir.AluOpType
ACT = mybir.ActivationFunctionType

B = 2048
DIM = 16
NF = 50
ND = 16
TILE = 128
TPC = 4
CHUNK = TILE * TPC
NCH = B // CHUNK
NTILES = B // TILE
Q = 4
SPQ = TILE // Q
HALF = SPQ // 2
HB = Q * HALF
SCALE = 16.0

ROWS = [125000, 1000, 125000, 1000, 125000, 1000, 1000, 1000, 1250, 125000, 125000, 1250, 12500,
        125000, 1000, 125000, 1250, 1000, 125000, 1250, 1000, 125000, 1000, 1250, 125000, 1250,
        12500, 12500, 12500, 1000, 1250, 125000, 125000, 1000, 12500, 1250, 1000, 1250, 1000,
        125000, 1000, 125000, 1250, 1250, 1000, 12500, 12500, 1250, 1000, 1250]
SMALL_SIZES = (1000, 1250)
SMALL = [f for size in SMALL_SIZES for f in range(NF) if ROWS[f] == size]
BIG = [f for f in range(NF) if ROWS[f] not in SMALL_SIZES]
FIELD = SMALL + BIG
NS, NB = len(SMALL), len(BIG)
TP = 125
KS = [ROWS[f] // TP for f in SMALL]
KOFF = [sum(KS[:j]) for j in range(NS)]
KSUM = sum(KS)
KMAX = max(KS)
GRP = 4
NG = -(-NS // GRP)
PR = 2
SLICES = [KS[q * GRP] // PR for q in range(NG)]
SOFF = [sum(SLICES[:q]) for q in range(NG + 1)]
NSL = SOFF[NG]
RING = 6
assert NSL % RING == 0 and all(KS[j] == PR * SLICES[j // GRP] for j in range(NS))
WSCALE = 64.0
JJ = NF // 2
JS = NS // 2
WORDS = 2 * DIM

ST = 11
TOP = 5
PIECES = []
_p = 0
for _g in range(4):
    _r = ST * _g + TOP + 1
    PIECES.append((_r, NF - _r, ST * _g, ST, _p, 0))
    _p += NF - _r
TOP_P = _p
for _g in range(5):
    PIECES.append((ST * _g + 1, TOP, ST * _g, TOP, TOP_P + TOP * (_g // 2), TOP * (_g % 2)))
DENSE_P = TOP_P + 3 * TOP
DENSE_R = 2
DENSE_K = ND // DENSE_R
KP = DENSE_P + DENSE_R
NCOL = NF - 1
HID1, HID2 = 512, 256
N1, N2 = HID1 // 128, HID2 // 128
PLOADS = 4
PB = [sum(KS[:min(NS, i * GRP * NG // PLOADS)]) for i in range(PLOADS + 1)]

ALL_SLICES = [(q, k) for q in range(NG) for k in range(SLICES[q])]
SPREAD = ((0, 0, 1, 2, 1, 2, 1, 2),) * (TPC - 1) + ((0, 0, 2, 2, 3, 2, 0, 0),)
PER_SLOT = NSL // TPC
EARLY = 4
assert all(sum(s) == PER_SLOT for s in SPREAD)


def slices_of(t, g):
    first = t * PER_SLOT + sum(SPREAD[t][:g])
    return ALL_SLICES[first:first + SPREAD[t][g]]


IDS_AHEAD = 3
LOAD_TURN = NG - IDS_AHEAD
IDS_BUFS = 4
MOVES = ((), (), (0,), (1,), (2, 3), (4,), (5,), (6, 7))

PIECE_INC = 16 * len(PIECES)
GATHER_INC = 16 * NB
FEED = 6
L1_MM = N1 * ST * 3
GRAM_CREDIT = 16
EVAC_CREDIT = 2
MLP_CREDIT = 8
MLPE_CREDIT = 4
HOT_CREDIT = RING
Z_CREDIT = 2
OH_CREDIT = 1


def tables_of(q):
    return range(q * GRP, min(NS, (q + 1) * GRP))


def build(nc, small, big, ids_small, ids_sample, ids_big, dense, w1, b1, w2, b2, w3, y):
    ctx = ExitStack()
    with ctx:
        def sb(name, shape, dt):
            return ctx.enter_context(nc.sbuf_tensor(name, shape, dt))

        def sem(name):
            return ctx.enter_context(nc.semaphore(name))

        ids16_dram = nc.dram_tensor("ids16_dram", (NCH * NS, CHUNK), F16).ap()

        parts = sb("parts", [128, KSUM, 2, DIM], F16)
        w1_sb = sb("w1_sb", [128, ST, 2, HID1], F16)
        w2_sb = sb("w2_sb", [128, N1, HID2], F32)
        w3_sb = sb("w3_sb", [128, N2, 128], F32)
        w3_in = sb("w3_in", [128, N2], F32)
        b1_sb = sb("b1_sb", [128, N1], F32)
        b2_sb = sb("b2_sb", [128, N2], F32)
        rows = sb("rows", [128, len(SMALL_SIZES), KMAX // PR], F32)
        odd = sb("odd", [128, TPC, NS], I32)
        ids_bc = sb("ids_bc", [128, IDS_BUFS, GRP, CHUNK], F16)
        onehot = sb("onehot", [128, RING, GRP, CHUNK], F16)
        looked = sb("looked", [128, NG, 2, TPC, 2, PR, WORDS], F16)
        gidx = sb("gidx", [128, TPC, NB], I32)
        emb = sb("emb", [128, TPC, NB, DIM], F32)
        split = sb("split", [128, TPC, JJ, 3, DIM, 2], F16)
        TLEN = SPQ * NF
        turned = sb("turned", [128, 2, TLEN + 80], F16)
        turned2 = sb("turned2", [128, 2, TLEN + 80], F16)
        diag = sb("diag", [128, 2, HALF, Q, NF], F16)
        gram = sb("gram", [128, 2, NCOL * HB], F32)
        z_both = sb("z_both", [128, 2, 2 * ST * TILE], F32)
        z = z_both[:, 0, :].rearrange("p (i k b) -> p i k b", i=2, b=TILE)
        z_parts = z_both[:, 1, :].bitcast(F16).rearrange("p (i s k b) -> p i s k b", i=2, s=2, b=TILE)
        h1 = sb("h1", [128, N1, TILE], F32)
        h2 = sb("h2", [128, N2, TILE], F32)
        y_sb = sb("y_sb", [1, 2, TILE], F32)

        stage = gram[:, :, :].rearrange("p a n -> p (a n)")
        w1_f32 = z_both[0:KP, :, :].rearrange("p a n -> p (a n)").rearrange("p (k n) -> p k n", n=HID1)
        small_f32 = stage[0:TP, 0:KSUM * DIM].rearrange("p (k d) -> p k d", d=DIM)
        after = KSUM * DIM
        ids_i32 = stage[0:NCH * NS, after:after + CHUNK].bitcast(I32)
        pair_i32 = stage[0:NCH * NS, after + CHUNK:after + 2 * CHUNK].bitcast(I32)
        ids16 = stage[0:NCH * NS, after + 2 * CHUNK:after + 2 * CHUNK + CHUNK // 2].bitcast(F16)

        gram_ps = [ctx.enter_context(nc.psum_tensor(f"gram_ps{i}", [128, 2, 512], F32)) for i in range(2)]
        look_ps = ctx.enter_context(nc.psum_tensor("look_ps", [128, 2, 512], F32))
        mlp_ps = [ctx.enter_context(nc.psum_tensor(f"mlp_ps{i}", [128, N1, TILE], F32)) for i in range(2)]

        ids_in = sem("ids_in")
        sample_in = sem("sample_in")
        small_in = [sem(f"small_in{i}") for i in range(PLOADS)]
        pairs_made = sem("pairs_made")
        ids_cast = sem("ids_cast")
        ids_saved = sem("ids_saved")
        odd_made = sem("odd_made")
        weights_in = sem("weights_in")
        rows_made = sem("rows_made")
        cleared = sem("cleared")
        hi_made = sem("hi_made")
        parts_ready = sem("parts_ready")
        gidx_in = [sem(f"gidx_in{t}") for t in range(TPC)]
        gathered = [sem(f"gathered{t}") for t in range(TPC)]
        gathers_begun = sem("gathers_begun")
        emb_read = sem("emb_read")
        ids_bc_in = [sem(f"ids_bc_in{i}") for i in range(IDS_BUFS)]
        onehot_ready = sem("onehot_ready")
        onehot_used = sem("onehot_used")
        looked_ready = sem("looked_ready")
        picks_begun = sem("picks_begun")
        picked = sem("picked")
        moved = sem("moved")
        dve_step = sem("dve_step")
        turned_ready = sem("turned_ready")
        diag_ready = sem("diag_ready")
        gram_done = sem("gram_done")
        gram_copied = sem("gram_copied")
        w1_hi = sem("w1_hi")
        w1_lo = sem("w1_lo")
        w1_ready = sem("w1_ready")
        z_hi = sem("z_hi")
        z_split = sem("z_split")
        packed = [sem(f"packed{h}") for h in range(2)]
        packs_begun = sem("packs_begun")
        dense_in = [sem(f"dense_in{i}") for i in range(2)]
        mlp_done = sem("mlp_done")
        mlp_copied = sem("mlp_copied")
        y_out = [sem(f"y_out{i}") for i in range(2)]

        block = ctx.enter_context(nc.Block())


        @block.sync
        def _(sp):
            def load_ids_bc(n, q):
                src = ids_of(n, q)
                if q >= IDS_BUFS:
                    sp.wait_ge(onehot_ready, n * NSL + SOFF[q - IDS_BUFS + 1])
                else:
                    sp.wait_ge(onehot_ready, n * NSL + (SOFF[NG + q - IDS_BUFS + 1] - NSL))
                put_ids_bc(src, q)

            def ids_of(n, q):
                cnt = len(tables_of(q))
                return ids16_dram[bass.ds(n * NS + q * GRP, cnt), :].unsqueeze(0).broadcast_to([TP, cnt, CHUNK])

            def put_ids_bc(src, q):
                sp.dma_start(ids_bc[0:TP, q % IDS_BUFS, 0:len(tables_of(q)), :], src)\
                  .then_inc(ids_bc_in[q % IDS_BUFS], 16)

            def load_sample_ids(n, first=False):
                src = ids_sample[bass.ds(n, 1), :, :, :].rearrange("a p t f -> (a p) t f")
                if not first:
                    sp.wait_ge(picked, n * NG)
                sp.dma_start(odd[:, :, :], src).then_inc(sample_in, 16)

            def pack(c, t, h):
                if h == 0:
                    sp.wait_ge(z_split, c * TPC + (t - 1 + Z_CREDIT))
                    sp.sem_inc(packs_begun, 1)
                sp.wait_ge(gram_copied, c * (8 * TPC) + (8 * t + 4 * h + 4 + EVAC_CREDIT))
                src = gram[:, h, :].rearrange("p (j b) -> p j b", b=HB)
                for r0, nr, c0, ncol, p0, k0 in PIECES:
                    sp.dma_start(z[p0:p0 + nr, t % 2, k0:k0 + ncol, h * HB:(h + 1) * HB],
                                 src[r0:r0 + nr, c0:c0 + ncol, :]).then_inc(packed[h], 16)
                if h == 0:
                    sp.dma_start(z[DENSE_P:KP, t % 2, 0:DENSE_K, :],
                                 dense[:, :, bass.ds(c * CHUNK + t * TILE, TILE)]).then_inc(dense_in[t % 2], 16)

            def load_gidx(n, t, first=False):
                src = ids_big[bass.ds(n * TPC + t, 1), :, :].rearrange("a p f -> (a p) f")
                if not first:
                    sp.wait_ge(gathered[t], n * GATHER_INC)
                sp.dma_start(gidx[:, t, :], src).then_inc(gidx_in[t], 16)

            def half_slot(c, i, before, load, last=False):
                if i == 0 and not last:
                    load_sample_ids(c + 1)
                if load:
                    if i < LOAD_TURN:
                        load_ids_bc(c + 1, i + IDS_AHEAD)
                    else:
                        load_ids_bc(c + 2, i - LOAD_TURN)
                if before or i >= 2:
                    pack(c, i // 2 - 1, i % 2)
                if i % 2 == 1 and (load or not last):
                    load_gidx(c + 1, i // 2)

            sp.dma_start(ids_i32, ids_small).then_inc(ids_in, 16)
            load_gidx(0, 0, first=True)
            sp.dma_start(small_f32[:, 0:PB[1], :], small[:, 0:PB[1], :]).then_inc(small_in[0], 16)
            for t in range(1, TPC):
                load_gidx(0, t, first=True)
            sp.wait_ge(ids_cast, 1)
            sp.dma_start(ids16_dram, ids16).then_inc(ids_saved, 16)
            for i in range(1, PLOADS):
                sp.dma_start(small_f32[:, PB[i]:PB[i + 1], :], small[:, PB[i]:PB[i + 1], :]).then_inc(small_in[i], 16)
            sp.wait_ge(ids_saved, 16)
            for q in range(IDS_BUFS):
                put_ids_bc(ids_of(0, q), q)
            load_sample_ids(0, first=True)
            for s, d in ((w1_f32, w1), (w2_sb[:, :, :], w2), (b1_sb[:, :], b1), (b2_sb[:, :], b2),
                         (w3_in[:, :], w3)):
                sp.dma_start(s, d).then_inc(weights_in, 16)
            for i in range(2):
                sp.sem_inc(packed[i], PIECE_INC)
            for q in range(IDS_BUFS, NG):
                load_ids_bc(0, q)
            for q in range(IDS_AHEAD):
                load_ids_bc(1, q)
            for i in range(LOAD_TURN):
                if i == 2:
                    sp.wait_ge(w1_ready, 1)
                half_slot(0, i, False, True)
            with sp.Fori(0, NCH - 2) as c:
                for i in range(LOAD_TURN, 2 * TPC):
                    half_slot(c, i, True, True)
                for i in range(LOAD_TURN):
                    half_slot(c + 1, i, True, True)
            for i in range(LOAD_TURN, 2 * TPC):
                half_slot(NCH - 2, i, True, False)
            for i in range(2 * TPC):
                half_slot(NCH - 1, i, True, False, last=True)
            for h in range(2):
                pack(NCH - 1, TPC - 1, h)

        @block.gpsimd
        def _(pool):
            def gathers(c, reuse):
                for t in range(TPC):
                    pool.wait_ge(gidx_in[t], c * 16 + 16)
                    if reuse:
                        pool.wait_ge(emb_read, c * TPC + (t + 1 - TPC))
                    pool.sem_inc(gathers_begun, 1)
                    for f in range(NB):
                        pool.indirect_dma_start(
                            emb[:, t, f, :], None, big[f],
                            bass.IndirectOffsetOnAxis(ap=gidx[:, t, f:f + 1], axis=0)).then_inc(gathered[t], 16)

            for s in range(len(SMALL_SIZES)):
                k = SMALL_SIZES[s] // TP // PR
                last = nc.gpsimd.iota(rows[0:TP, s, 0:k], [[1, k]], base=0, channel_multiplier=k,
                                      allow_small_or_imprecise_dtypes=True)
            last.then_inc(rows_made, 1)
            gathers(0, False)
            with pool.Fori(1, NCH) as c:
                gathers(c, True)

        @block.vector
        def _(dve):
            def compare(n, q, k):
                if k == 0:
                    dve.wait_ge(ids_bc_in[q % IDS_BUFS], n * (16 * NG // IDS_BUFS) + 16 * (q // IDS_BUFS + 1))
                dve.wait_ge(onehot_used, n * NSL + (SOFF[q] + k + 1 - RING + HOT_CREDIT))
                cnt = len(tables_of(q))
                size = SMALL_SIZES.index(ROWS[SMALL[q * GRP]])
                nc.vector.tensor_scalar(onehot[0:TP, (SOFF[q] + k) % RING, 0:cnt, :],
                                        ids_bc[0:TP, q % IDS_BUFS, 0:cnt, :],
                                        rows[0:TP, size, k:k + 1], None, ALU.is_equal).then_inc(onehot_ready, 1)

            def pick(n, q):
                if q == 0:
                    dve.wait_ge(odd_made, n + 1)
                dve.wait_ge(looked_ready, n * NG + (q + 1 + OH_CREDIT))
                cnt = len(tables_of(q))
                dve.sem_inc(picks_begun, 1)
                for h in range(-(-cnt // 2)):
                    na = min(2, cnt - 2 * h)
                    both = looked[:, q, h, :, 0:na, :, :].bitcast(U32)
                    first = q * GRP + 2 * h
                    mask = odd[:, :, first:first + na].unsqueeze(3)\
                        .broadcast_to([128, TPC, na, WORDS // 2])
                    last = nc.vector.copy_predicated(both[:, :, :, 0, :], mask, both[:, :, :, 1, :])
                last.then_inc(picked, 1)

            def find_odd(n):
                dve.wait_ge(sample_in, n * 16 + 16)
                nc.vector.tensor_scalar(odd[:, :, :], odd[:, :, :], 1, None, ALU.bitwise_and).then_inc(odd_made, 1)

            def compare_and_pick(n, s):
                if s == RING:
                    find_odd(n)
                q, k = ALL_SLICES[s]
                compare(n, q, k)
                if s - RING in SOFF[1:]:
                    pick(n, SOFF.index(s - RING) - 1)

            def split_products(c, t):
                dve.wait_ge(z_hi, c * TPC + (t + 1))
                nc.vector.tensor_tensor(z_parts[0:KP, t % 2, 1, :, :], z[0:KP, t % 2, :, :],
                                        z_parts[0:KP, t % 2, 0, :, :], ALU.subtract).then_inc(z_split, 1)

            STEPS = 3

            def split_rows(c, t):
                dve.wait_ge(gathered[t], c * GATHER_INC + GATHER_INC)

                def of_parity(a):
                    j0 = JS + 1 - a
                    e = emb[:, t, 1 - a:NB:2, :]
                    return e, split[:, t, j0:JJ, 0, :, a], split[:, t, j0:JJ, 1, :, a]

                for a in range(2):
                    e, hi, lo = of_parity(a)
                    nc.vector.tensor_scalar(hi, e, SCALE, None, ALU.mult).then_inc(dve_step, 1)
                dve.wait_ge(dve_step, c * (STEPS * TPC) + (STEPS * t + 2))
                e, hi, lo = of_parity(0)
                nc.vector.scalar_tensor_tensor(lo, e, SCALE, hi, ALU.mult, ALU.subtract)
                e, hi, lo = of_parity(1)
                nc.vector.scalar_tensor_tensor(lo, e, SCALE, hi, ALU.mult, ALU.subtract).then_inc(emb_read, 1)
                if t == 0:
                    dve.wait_ge(moved, c + 1)
                nc.vector.tensor_copy(
                    split[:, t, JS:JJ, 2, :, :].rearrange("p j d a -> p j (d a)"),
                    split[:, t, JS:JJ, 0, :, :].rearrange("p j d a -> p j (d a)")).then_inc(dve_step, 1)

            def turn(c, t):
                dve.wait_ge(dve_step, c * (STEPS * TPC) + (STEPS * t + 3))
                dve.wait_ge(gram_done, c * (8 * TPC) + (8 * t + GRAM_CREDIT - 8))
                src = split[:, t, :, :, :, :].rearrange("p j s d a -> p j (s d a)").bitcast(U32)
                for buf, w0 in ((turned, 0), (turned2, DIM)):
                    out = buf[:, t % 2, 0:TLEN].bitcast(U32).rearrange("p (b j) -> p j b", j=JJ)
                    nc.vector.transpose(out, src[:, :, w0:w0 + WORDS]).then_inc(turned_ready, 1)

            def set_out(c, t, h):
                if h == 0:
                    dve.wait_ge(turned_ready, c * (2 * TPC) + (2 * t + 2))
                dve.wait_ge(gram_done, c * (8 * TPC) + (8 * t + 4 * h + GRAM_CREDIT - 4))
                for r in range(Q):
                    p = slice(32 * r, 32 * r + 32)
                    last = nc.vector.tensor_copy(
                        diag[p, h, :, r, :].bitcast(U32),
                        turned[p, t % 2, h * HALF * NF:(h + 1) * HALF * NF].bitcast(U32)
                        .rearrange("p (b j) -> p b j", j=JJ))
                last.then_inc(diag_ready, 1)

            def slot(c, t, before, more):
                mine = range(t * PER_SLOT, (t + 1) * PER_SLOT)
                if more:
                    for s in mine[:EARLY]:
                        compare_and_pick(c + 1, s)
                if before or t >= 1:
                    set_out(c, t - 1, 1)
                if not more:
                    split_products(c, t - 2)
                split_rows(c, t)
                turn(c, t)
                if more:
                    for s in mine[EARLY:]:
                        compare_and_pick(c + 1, s)
                set_out(c, t, 0)
                if more and (before or t >= 2):
                    split_products(c, t - 2)
                if more and t == TPC - 1:
                    for q in range(NG):
                        if SOFF[q + 1] + RING >= NSL:
                            pick(c + 1, q)

            dve.sem_inc(z_split, Z_CREDIT)
            nc.vector.memset(w3_sb[:, :, :], 0.0)
            nc.vector.memset(turned[:, :, TLEN:], 0.0)
            nc.vector.memset(turned2[:, :, TLEN:], 0.0)
            dve.wait_ge(ids_in, 16)
            nc.vector.tensor_scalar(pair_i32, ids_i32, 1, None, ALU.logical_shift_right).then_inc(pairs_made, 1)
            dve.wait_ge(pairs_made, 1)
            nc.vector.tensor_copy(ids16, pair_i32).then_inc(ids_cast, 1)
            nc.vector.memset(diag[:, :, :, :, :], 0.0).then_inc(cleared, 1)
            dve.wait_ge(rows_made, 1)
            for s in range(NSL):
                i = SOFF.index(s) * PLOADS // NG if s in SOFF and SOFF.index(s) * PLOADS % NG == 0 else None
                if i is not None:
                    dve.wait_ge(hi_made, i + 1)
                    piece = slice(PB[i], PB[i + 1])
                    nc.vector.scalar_tensor_tensor(parts[0:TP, piece, 1, :], small_f32[:, piece, :], SCALE,
                                                   parts[0:TP, piece, 0, :], ALU.mult, ALU.subtract)\
                        .then_inc(parts_ready, 1)
                compare_and_pick(0, s)
            for q in range(NG):
                if SOFF[q + 1] + RING >= NSL:
                    pick(0, q)
            for t in range(TPC):
                slot(0, t, False, True)
                if t == 0:
                    dve.wait_ge(w1_hi, 1)
                    nc.vector.tensor_copy(w3_sb[:, :, 0], w3_in[:, :])
                    nc.vector.scalar_tensor_tensor(w1_sb[0:KP, :, 1, :], w1_f32, WSCALE, w1_sb[0:KP, :, 0, :],
                                                   ALU.mult, ALU.subtract).then_inc(w1_lo, 1)
                    dve.wait_ge(w1_lo, 1)
                    nc.vector.memset(z[96:128, :, :, :], 0.0).then_inc(w1_ready, 1)
            with dve.Fori(1, NCH - 1) as c:
                for t in range(TPC):
                    slot(c, t, True, True)
            for t in range(TPC):
                slot(NCH - 1, t, True, False)
            set_out(NCH - 1, TPC - 1, 1)
            split_products(NCH - 1, TPC - 2)
            split_products(NCH - 1, TPC - 1)

        @block.tensor
        def _(pe):
            def look_up(n, q, k):
                if k == 0:
                    pe.wait_ge(looked_ready, n * NG + (q + OH_CREDIT))
                pe.wait_ge(onehot_ready, n * NSL + (SOFF[q] + k + 1))
                js = tables_of(q)
                width = PR * WORDS
                for j in js:
                    first = j % 2 == 0
                    for t in range(TPC):
                        at = (t * 2 + j % 2) * width
                        last = nc.tensor.matmul(
                            look_ps[:, j % GRP // 2, at:at + width],
                            onehot[0:TP, (SOFF[q] + k) % RING, j % GRP, t * TILE:(t + 1) * TILE],
                            parts[0:TP, KOFF[j] + PR * k:KOFF[j] + PR * (k + 1), :, :].rearrange("p i s d -> p (i s d)"),
                            start=(k == 0 and first and t == 0),
                            stop=(k == SLICES[q] - 1), skip_group_check=True)
                last.then_inc(onehot_used, 1)

            def dots(c, t, g):
                if g % 4 == 0:
                    pe.wait_ge(diag_ready, c * (2 * TPC) + (2 * t + g // 4 + 1))
                pe.wait_ge(gram_copied, c * (8 * TPC) + (8 * t + g + EVAC_CREDIT - 1))
                for i in range(4):
                    b = 4 * g + i
                    o = gram_ps[g % 2][:, i // 2, (i % 2) * Q * NF:(i % 2 + 1) * Q * NF]
                    moving = diag[:, g // 4, b % HALF, :, :].rearrange("p r n -> p (r n)")
                    nc.tensor.matmul(o, turned[:, t % 2, b * NF:b * NF + 128], moving, start=True, stop=False)
                    last = nc.tensor.matmul(o, turned2[:, t % 2, b * NF:b * NF + 128], moving,
                                            start=False, stop=True)
                last.then_inc(gram_done, 1)

            def mlp(c, t, g):
                if g < FEED:
                    if g == 0:
                        pe.wait_ge(z_split, c * TPC + (t + 1 + Z_CREDIT))
                    if g % (FEED // 2) == 0:
                        pe.wait_ge(mlp_copied, c * (4 * TPC) + (4 * t + g * 2 // FEED - 1 + MLPE_CREDIT))
                    for i in range(g * L1_MM // FEED, (g + 1) * L1_MM // FEED):
                        n, k = i // (3 * ST), i // 3 % ST
                        w, x = ((0, 0), (0, 1), (1, 0))[i % 3]
                        last = nc.tensor.matmul(mlp_ps[n // 2][:, n % 2, :], w1_sb[0:KP, k, w, n * 128:(n + 1) * 128],
                                                z_parts[0:KP, t % 2, x, k, :], start=(k == 0 and w + x == 0),
                                                stop=(k == ST - 1 and w == 1))
                        if (i + 1) % (L1_MM // 2) == 0:
                            last.then_inc(mlp_done, 1)
                elif g == FEED:
                    pe.wait_ge(mlp_copied, c * (4 * TPC) + (4 * t + 2 + MLPE_CREDIT))
                    for o in range(N2):
                        for n in range(N1):
                            last = nc.tensor.matmul(mlp_ps[0][:, o, :],
                                                    w2_sb[:, n, o * 128:(o + 1) * 128], h1[:, n, :],
                                                    start=(n == 0), stop=(n == N1 - 1))
                    last.then_inc(mlp_done, 1)
                else:
                    pe.wait_ge(mlp_copied, c * (4 * TPC) + (4 * t + 3 + MLPE_CREDIT))
                    for o in range(N2):
                        last = nc.tensor.matmul(mlp_ps[1][:, 0, :], w3_sb[:, o, :], h2[:, o, :],
                                                start=(o == 0), stop=(o == N2 - 1))
                    last.then_inc(mlp_done, 1)

            def slot(c, t, before, more):
                for g in range(8):
                    if before or t >= 1:
                        dots(c, t - 1, g)
                    if before or t >= 3:
                        mlp(c, t - 3, g)
                    if more:
                        for q, k in slices_of(t, g):
                            look_up(c + 1, q, k)

            pe.sem_inc(gram_done, GRAM_CREDIT)
            pe.sem_inc(mlp_done, MLP_CREDIT)
            pe.sem_inc(onehot_used, HOT_CREDIT)
            pe.wait_ge(cleared, 1)
            for q in range(NG):
                pe.wait_ge(parts_ready, q * PLOADS // NG + 1)
                for k in range(SLICES[q]):
                    look_up(0, q, k)
            for t in range(TPC):
                if t == 1:
                    pe.wait_ge(weights_in, 16 * 5)
                    pe.wait_ge(w1_ready, 1)
                slot(0, t, False, True)
            with pe.Fori(1, NCH - 1) as c:
                for t in range(TPC):
                    slot(c, t, True, True)
            for t in range(TPC):
                slot(NCH - 1, t, True, False)
            for g in range(8):
                mlp(NCH - 1, TPC - 3, g)
            for g in range(8):
                dots(NCH - 1, TPC - 1, g)
            for t in (TPC - 2, TPC - 1):
                for g in range(8):
                    mlp(NCH - 1, t, g)

        @block.scalar
        def _(act):
            def copy_dots(c, t, g):
                h = g // 4
                if g % 4 == 0:
                    act.wait_ge(packed[h], c * (TPC * PIECE_INC) + PIECE_INC * (t + 1))
                act.wait_ge(gram_done, c * (8 * TPC) + (8 * t + g + 1 + GRAM_CREDIT))
                src = gram_ps[g % 2][0:NF, :, 0:2 * Q * NF].rearrange("p k (b j) -> p j k b", j=NF)[:, 0:NCOL]
                out = gram[0:NF, h, :].rearrange("p (j b) -> p j b", b=HB)[:, :, (g % 4) * 16:(g % 4 + 1) * 16]\
                    .rearrange("p j (k b) -> p j k b", k=2)
                nc.scalar.activation(out, src, ACT.Copy, scale=1.0 / (SCALE * SCALE)).then_inc(gram_copied, 1)

            def copy_lookups(n, q, first=False):
                if q == 0 and not first:
                    act.wait_ge(moved, n)
                act.wait_ge(onehot_used, n * NSL + (SOFF[q + 1] + HOT_CREDIT))
                cnt = len(tables_of(q))
                if cnt == GRP:
                    src = look_ps[:, :, :]
                    out = looked[:, q, :, :, :, :, :].rearrange("p h t a i w -> p h (t a i w)")
                else:
                    src = look_ps[:, 0, :].rearrange("p (t w) -> p t w", t=TPC)[:, :, 0:PR * WORDS]
                    out = looked[:, q, 0, :, 0, :, :].rearrange("p t i w -> p t (i w)")
                nc.scalar.activation(out, src, ACT.Copy).then_inc(looked_ready, 1)

            def move(n, q, first=False):
                act.wait_ge(picked, n * NG + (q + 1))
                if q == 0 and not first:
                    act.wait_ge(turned_ready, n * (2 * TPC))
                cnt = len(tables_of(q))
                for h in range(-(-cnt // 2)):
                    j = (q * GRP) // 2 + h
                    na = min(2, cnt - 2 * h)
                    for s0, ns in ((0, 2), (2, 1)):
                        src = looked[:, q, h, :, 0:na, 0, 0:ns * DIM].rearrange("p t a w -> p t w a")
                        last = nc.scalar.activation(
                            split[:, :, j, s0:s0 + ns, :, 0:na].rearrange("p t s d a -> p t (s d) a"), src, ACT.Copy)
                if q == NG - 1:
                    last.then_inc(moved, 1)

            def split_products(c, t):
                for h in range(2):
                    act.wait_ge(packed[h], c * (TPC * PIECE_INC) + PIECE_INC * (t + 2))
                act.wait_ge(dense_in[t % 2], c * (16 * TPC // 2) + 16 * (t // 2 + 1))
                act.wait_ge(mlp_done, c * (4 * TPC) + (4 * (t - 2) + 2 + MLP_CREDIT))
                nc.scalar.activation(z_parts[0:KP, t % 2, 0, :, :], z[0:KP, t % 2, :, :], ACT.Copy).then_inc(z_hi, 1)

            def copy_mlp(c, t, g):
                done = c * (4 * TPC) + (4 * t + MLP_CREDIT)
                if g in (FEED // 2 - 1, FEED - 1):
                    part = g * 2 // FEED
                    act.wait_ge(mlp_done, done + (part + 1))
                    for n in (2 * part, 2 * part + 1):
                        ins = nc.scalar.activation(h1[:, n, :], mlp_ps[part][:, n % 2, :], ACT.Relu, bias=b1_sb[:, n:n + 1],
                                                   scale=1.0 / WSCALE)
                    ins.then_inc(mlp_copied, 1)
                elif g == FEED:
                    act.wait_ge(mlp_done, done + 3)
                    for o in range(N2):
                        ins = nc.scalar.activation(h2[:, o, :], mlp_ps[0][:, o, :],
                                                   ACT.Relu, bias=b2_sb[:, o:o + 1])
                    ins.then_inc(mlp_copied, 1)
                elif g > FEED:
                    act.wait_ge(mlp_done, done + 4)
                    act.wait_ge(y_out[t % 2], c * (16 * TPC // 2) + (16 * (t // 2) + 16))
                    nc.scalar.activation(y_sb[0:1, t % 2, :].rearrange("p (r b) -> p b r", r=Q),
                                         mlp_ps[1][0:1, 0, :].rearrange("p (b r) -> p b r", r=Q),
                                         ACT.Copy).then_inc(mlp_copied, 1)
                    act.wait_ge(mlp_copied, c * (4 * TPC) + (4 * t + 4 + MLPE_CREDIT))
                    act.dma_start(y[:, bass.ds(c * CHUNK + t * TILE, TILE)], y_sb[0:1, t % 2, :])\
                        .then_inc(y_out[t % 2], 16)

            def slot(c, t, before, more):
                for g in range(8):
                    if before or t >= 1:
                        copy_dots(c, t - 1, g)
                    if before or t >= 3:
                        copy_mlp(c, t - 3, g)
                    if more:
                        for q, k in slices_of(t, g):
                            if k == SLICES[q] - 1:
                                copy_lookups(c + 1, q)
                        if t == TPC - 1:
                            for q in MOVES[g]:
                                move(c + 1, q)
                    if g == 4 and (before or t >= 2):
                        split_products(c, t - 2)

            act.sem_inc(gram_copied, EVAC_CREDIT)
            act.sem_inc(mlp_copied, MLPE_CREDIT)
            act.sem_inc(looked_ready, OH_CREDIT)
            for i in range(2):
                act.sem_inc(y_out[i], 16)
            for i in range(PLOADS):
                act.wait_ge(small_in[i], 16)
                piece = slice(PB[i], PB[i + 1])
                nc.scalar.activation(parts[0:TP, piece, 0, :], small_f32[:, piece, :], ACT.Copy, scale=SCALE)\
                    .then_inc(hi_made, 1)
            for q in range(NG):
                copy_lookups(0, q, first=True)
                if q == NG // 2:
                    act.wait_ge(weights_in, 16 * 5)
                    nc.scalar.activation(w1_sb[0:KP, :, 0, :], w1_f32, ACT.Copy, scale=WSCALE).then_inc(w1_hi, 1)
            for q in range(NG):
                move(0, q, first=True)
            act.wait_ge(parts_ready, PLOADS)
            act.wait_ge(ids_saved, 16)
            for t in range(TPC):
                slot(0, t, False, True)
            with act.Fori(1, NCH - 1) as c:
                for t in range(TPC):
                    slot(c, t, True, True)
            for t in range(TPC):
                slot(NCH - 1, t, True, False)
            for g in range(8):
                copy_mlp(NCH - 1, TPC - 3, g)
            for g in range(8):
                copy_dots(NCH - 1, TPC - 1, g)
                if g == 3:
                    split_products(NCH - 1, TPC - 2)
            for g in range(8):
                copy_mlp(NCH - 1, TPC - 2, g)
            split_products(NCH - 1, TPC - 1)
            for g in range(8):
                copy_mlp(NCH - 1, TPC - 1, g)
            for i in range(2):
                act.wait_ge(y_out[i], 16 * (NTILES // 2 + 1))


def pair_rows():
    zero = NF * (NF - 1) // 2 + ND
    at = np.full((KP, ST), zero)
    seen = 0
    for r0, nr, c0, ncol, p0, k0 in PIECES:
        for r in range(nr):
            for k in range(ncol):
                if c0 + k < r0 + r:
                    i, j = sorted((FIELD[c0 + k], FIELD[r0 + r]))
                    at[p0 + r, k0 + k] = i * (2 * NF - i - 1) // 2 + j - i - 1
                    seen += 1
    assert seen == NF * (NF - 1) // 2
    for d in range(ND):
        at[DENSE_P + d // DENSE_K, d % DENSE_K] = NF * (NF - 1) // 2 + d
    return at


def kernel(**inputs):
    import concourse.bacc as bacc
    from concourse.bass_utils import run_bass_kernel_spmd

    a = {k: np.asarray(v) for k, v in inputs.items()}
    ids = a["ids"]
    small = np.concatenate([a[f"tbl_{f}"].reshape(TP, -1) for f in SMALL], axis=1).reshape(TP, KSUM, DIM)
    w1 = np.concatenate([a["W_top1"], np.zeros((1, HID1), np.float32)])[pair_rows()]
    dense = a["dense_ctx"].reshape(B // TILE, Q, SPQ, ND).transpose(3, 0, 2, 1).reshape(DENSE_R, DENSE_K, B)
    by_chunk = ids[:, SMALL].reshape(NCH, CHUNK, NS).transpose(0, 2, 1).reshape(NCH * NS, CHUNK)
    arrays = {
        "small": small,
        "ids_small": by_chunk,
        "ids_sample": ids[:, SMALL].reshape(NCH, TPC, TILE, NS).transpose(0, 2, 1, 3),
        "ids_big": ids[:, BIG].reshape(NTILES, TILE, NB),
        "dense": dense,
        "w1": w1,
        "b1": a["b_top1"].reshape(N1, 128).T,
        "w2": a["W_top2"].reshape(N1, 128, HID2).transpose(1, 0, 2),
        "b2": a["b_top2"].reshape(N2, 128).T,
        "w3": a["W_top3"].reshape(N2, 128).T,
    }
    for f in BIG:
        arrays[f"tbl_{f}"] = a[f"tbl_{f}"]
    arrays = {k: np.ascontiguousarray(v) for k, v in arrays.items()}
    nc = bacc.Bacc("TRN2", target_bir_lowering=False, num_devices=1)
    ap = {k: nc.dram_tensor(k, v.shape, mybir.dt.from_np(v.dtype), kind="ExternalInput").ap()
          for k, v in arrays.items()}
    y = nc.dram_tensor("y", (1, B), F32, kind="ExternalOutput").ap()
    build(nc, ap["small"], [ap[f"tbl_{f}"] for f in BIG], ap["ids_small"], ap["ids_sample"], ap["ids_big"], ap["dense"],
          ap["w1"], ap["b1"], ap["w2"], ap["b2"], ap["w3"], y)
    r = run_bass_kernel_spmd(nc, [arrays], core_ids=[0])
    return r.results[0]["y"].reshape(B, 1)
```
